# Optimizing a Trainium2 kernel written in Bass

```python
import numpy as np
import jax
import jax.numpy as jnp

def _softmax(x, axis=-1):
    return jax.nn.softmax(x, axis=axis)

def _gelu(x):
    return jax.nn.gelu(x, approximate=True)

def _silu(x):
    return jax.nn.silu(x)

def _sigmoid(x):
    return jax.nn.sigmoid(x)

def _layernorm(x, axis=-1, eps=1e-05):
    m = jnp.mean(x, axis=axis, keepdims=True)
    v = jnp.var(x, axis=axis, keepdims=True)
    return (x - m) / jnp.sqrt(v + eps)

def _scatter_add(tgt, idx, src, axis=0):
    return tgt.at[idx].add(src)

def _segment_sum(src, seg, n):
    return jax.ops.segment_sum(src, seg, n)
kernel_name = 'mk_xattn_ffn_d2_seqx_r8_5b5e0f'

def setup_inputs(seed: int=0):
    np.random.seed(seed)
    _w = jnp.asarray

    def _rec_inputs():
        import jax
        import jax.numpy as jnp
        _rk = jax.random.key(seed)
        x = 7.22e-05 + 1 * jax.random.normal(jax.random.fold_in(_rk, 1), (16, 256, 128), jnp.float32)
        _lenS = 256 - jax.random.randint(jax.random.fold_in(_rk, 7), (16,), 0, max(1, 256 // 4) + 1, jnp.int32)
        _lenS2 = 64 - jax.random.randint(jax.random.fold_in(_rk, 8), (16,), 0, max(1, 64 // 4) + 1, jnp.int32)
        _ctx_1024P = jax.random.normal(jax.random.fold_in(_rk, 11), (16, 16, 128), jnp.float32)
        _ctx_1024c = jax.random.dirichlet(jax.random.fold_in(_rk, 511), 0.3 * jnp.ones((16,), jnp.float32), (16, 64))
        _ctx_1024t = jnp.einsum('bsk,bkd->bsd', _ctx_1024c, _ctx_1024P)
        _ctx_1024t = _ctx_1024t * jax.lax.rsqrt(jnp.mean(jnp.square(_ctx_1024t)) + 1e-12) * 0.953939
        ctx_1024 = -0.000514642 + 1.00011 * (_ctx_1024t + 0.3 * jax.random.normal(jax.random.fold_in(_rk, 611), (16, 64, 128), jnp.float32))
        return (x, ctx_1024)
    x, ctx_1024 = _rec_inputs()

    def _L0_xattn_setup():
        import jax, jax.numpy as jnp
        import numpy as np
        B, L_ENC, L_DEC, D = (16, 64, 128, 128)
        key = jax.random.key(seed)
        k1, k2, k3, k4, k5, k6 = jax.random.split(key, 6)
        encoder_hc = jax.random.normal(k1, (B, L_ENC, D), dtype=jnp.float32)
        decoder_hq = jax.random.normal(k2, (B, L_DEC, D), dtype=jnp.float32)
        w_sim = jax.random.normal(k3, (3 * D,), dtype=jnp.float32) * 0.02
        b_sim = jax.random.normal(k4, (1,), dtype=jnp.float32) * 0.02
        W_qv = jax.random.normal(k5, (4 * D, D), dtype=jnp.float32) * 0.02
        b_qv = jax.random.normal(k6, (D,), dtype=jnp.float32) * 0.02
        return {'encoder_hc': encoder_hc, 'decoder_hq': decoder_hq, 'w_sim': w_sim, 'b_sim': b_sim, 'W_qv': W_qv, 'b_qv': b_qv}
    _L0_xattn_all = _L0_xattn_setup()
    _L0_xattn_in = {k: v for k, v in _L0_xattn_all.items() if k in ('w_sim', 'b_sim', 'W_qv', 'b_qv')}
    del _L0_xattn_all

    def _L0_ffn_setup():
        import jax, jax.numpy as jnp
        import numpy as np
        D_MODEL = 128
        M = 64
        INNER = 16
        key = jax.random.key(seed)
        ks = jax.random.split(key, 9)

        def init(k, shape, fan_in):
            bound = 1.0 / np.sqrt(fan_in)
            return jax.random.uniform(k, shape, jnp.float32, -bound, bound)
        x = jax.random.normal(ks[0], (16, 512, D_MODEL), dtype=jnp.float32)
        Win = init(ks[1], (D_MODEL, M), D_MODEL)
        bin_ = init(ks[2], (M,), D_MODEL)
        W1 = init(ks[3], (M, INNER), 1)
        b1 = init(ks[4], (M, INNER), 1)
        W2 = init(ks[5], (M, INNER), INNER)
        b2 = init(ks[6], (M,), INNER)
        Wout = init(ks[7], (M, D_MODEL), M)
        bout = init(ks[8], (D_MODEL,), M)
        return {'x': x, 'Win': Win, 'bin_': bin_, 'W1': W1, 'b1': b1, 'W2': W2, 'b2': b2, 'Wout': Wout, 'bout': bout}
    _L0_ffn_all = _L0_ffn_setup()
    _L0_ffn_in = {k: v for k, v in _L0_ffn_all.items() if k in ('Win', 'bin_', 'W1', 'b1', 'W2', 'b2', 'Wout', 'bout')}
    del _L0_ffn_all

    def _L1_xattn_setup():
        import jax, jax.numpy as jnp
        import numpy as np
        B, S, H = (4, 256, 128)
        key = jax.random.key(seed)
        ks = jax.random.split(key, 6)
        scale = 1.0 / np.sqrt(H)
        return {'query': jax.random.normal(ks[0], (B, S, H), dtype=jnp.float32), 'key': jax.random.normal(ks[1], (B, S, H), dtype=jnp.float32), 'value': jax.random.normal(ks[2], (B, S, H), dtype=jnp.float32), 'WQ': jax.random.normal(ks[3], (H, H), dtype=jnp.float32) * scale, 'WK': jax.random.normal(ks[4], (H, H), dtype=jnp.float32) * scale, 'WV': jax.random.normal(ks[5], (H, H), dtype=jnp.float32) * scale}
    _L1_xattn_all = _L1_xattn_setup()
    _L1_xattn_in = {k: v for k, v in _L1_xattn_all.items() if k in ('WQ', 'WK', 'WV')}
    del _L1_xattn_all

    def _L1_ffn_setup():
        import jax, jax.numpy as jnp
        import numpy as np
        EPS = 1e-06
        LN_EPS = 1e-05

        def _absmean_core(W):
            gamma = jnp.mean(jnp.abs(W)) + EPS
            Ws = W / gamma
            Wq = jnp.sign(Ws) * jnp.minimum(jnp.round(jnp.abs(Ws)), 1.0)
            return (Wq, gamma)

        @jax.custom_vjp
        def absmean(W):
            return _absmean_core(W)[0]

        def _absmean_fwd(W):
            Wq, gamma = _absmean_core(W)
            return (Wq, gamma)

        def _absmean_bwd(gamma, g):
            return (g / gamma,)
        absmean.defvjp(_absmean_fwd, _absmean_bwd)

        def layernorm(x, w, b, eps=LN_EPS):
            mu = jnp.mean(x, axis=-1, keepdims=True)
            var = jnp.mean((x - mu) ** 2, axis=-1, keepdims=True)
            return (x - mu) * jax.lax.rsqrt(var + eps) * w + b
        key = jax.random.key(seed)
        k1, k2, k3 = jax.random.split(key, 3)
        d, h = (128, 512)
        B, T = (8, 256)
        return {'x': jax.random.normal(k1, (B, T, d), jnp.float32), 'W_fc': jax.random.normal(k2, (h, d), jnp.float32), 'ln_w': jnp.ones((h,), jnp.float32), 'ln_b': jnp.zeros((h,), jnp.float32), 'W_proj': jax.random.normal(k3, (d, h), jnp.float32)}
    _L1_ffn_all = _L1_ffn_setup()
    _L1_ffn_in = {k: v for k, v in _L1_ffn_all.items() if k in ('W_fc', 'ln_w', 'ln_b', 'W_proj')}
    del _L1_ffn_all
    return {'x': x, 'ctx_1024': ctx_1024, 'L0_xattn_w_sim': _L0_xattn_in['w_sim'], 'L0_xattn_b_sim': _L0_xattn_in['b_sim'], 'L0_xattn_W_qv': _L0_xattn_in['W_qv'], 'L0_xattn_b_qv': _L0_xattn_in['b_qv'], 'L0_ffn_Win': _L0_ffn_in['Win'], 'L0_ffn_bin_': _L0_ffn_in['bin_'], 'L0_ffn_W1': _L0_ffn_in['W1'], 'L0_ffn_b1': _L0_ffn_in['b1'], 'L0_ffn_W2': _L0_ffn_in['W2'], 'L0_ffn_b2': _L0_ffn_in['b2'], 'L0_ffn_Wout': _L0_ffn_in['Wout'], 'L0_ffn_bout': _L0_ffn_in['bout'], 'L1_xattn_WQ': _L1_xattn_in['WQ'], 'L1_xattn_WK': _L1_xattn_in['WK'], 'L1_xattn_WV': _L1_xattn_in['WV'], 'L1_ffn_W_fc': _L1_ffn_in['W_fc'], 'L1_ffn_ln_w': _L1_ffn_in['ln_w'], 'L1_ffn_ln_b': _L1_ffn_in['ln_b'], 'L1_ffn_W_proj': _L1_ffn_in['W_proj']}

def reference(x, ctx_1024, L0_xattn_w_sim, L0_xattn_b_sim, L0_xattn_W_qv, L0_xattn_b_qv, L0_ffn_Win, L0_ffn_bin_, L0_ffn_W1, L0_ffn_b1, L0_ffn_W2, L0_ffn_b2, L0_ffn_Wout, L0_ffn_bout, L1_xattn_WQ, L1_xattn_WK, L1_xattn_WV, L1_ffn_W_fc, L1_ffn_ln_w, L1_ffn_ln_b, L1_ffn_W_proj):
    import jax
    import jax.numpy as jnp

    def _L0_xattn_ref(encoder_hc, decoder_hq, w_sim, b_sim, W_qv, b_qv):
        import jax, jax.numpy as jnp
        import numpy as np
        B, L_ENC, L_DEC, D = (16, 64, 128, 128)
        d = encoder_hc.shape[-1]
        w1, w2, w3 = (w_sim[:d], w_sim[d:2 * d], w_sim[2 * d:])
        Sim = (encoder_hc @ w1)[:, :, None] + (decoder_hq @ w2)[:, None, :] + jnp.einsum('bid,bjd->bij', encoder_hc * w3, decoder_hq) + b_sim[0]
        A = jax.nn.softmax(Sim, axis=2)
        hq_hat = jnp.einsum('bij,bjd->bid', A, decoder_hq)
        Batt = jax.nn.softmax(jnp.max(Sim, axis=2), axis=1)
        hc_bar = jnp.einsum('bi,bid->bd', Batt, encoder_hc)[:, None, :]
        hc_hat = jnp.broadcast_to(hc_bar, encoder_hc.shape)
        feats = jnp.concatenate([encoder_hc, hq_hat, encoder_hc * hq_hat, encoder_hc * hc_hat], axis=-1)
        hcq = feats @ W_qv + b_qv
        return hcq

    def _L0_ffn_ref(x, Win, bin_, W1, b1, W2, b2, Wout, bout):
        import jax, jax.numpy as jnp
        import numpy as np
        D_MODEL = 128
        M = 64
        INNER = 16
        s = jnp.einsum('btd,dm->btm', x, Win) + bin_
        h = jax.nn.relu(s[..., None] * W1 + b1)
        g = jnp.einsum('btmh,mh->btm', h, W2) + b2
        out = jnp.einsum('btm,md->btd', g, Wout) + bout
        return out

    def _L1_xattn_ref(query, key, value, WQ, WK, WV):
        import jax, jax.numpy as jnp
        import numpy as np
        B, S, H = (4, 256, 128)
        q = jnp.einsum('bsh,oh->bso', query, WQ)
        k = jnp.einsum('bsh,oh->bso', key, WK)
        v = jnp.einsum('bsh,oh->bso', value, WV)
        hidden_size = q.shape[-1]
        scores = jnp.einsum('bqh,bkh->bqk', q, k) / jnp.sqrt(jnp.float32(hidden_size))
        attn = jax.nn.softmax(scores, axis=2)
        return jnp.einsum('bqk,bkh->bqh', attn, v)

    def _L1_ffn_ref(x, W_fc, ln_w, ln_b, W_proj):
        import jax, jax.numpy as jnp
        import numpy as np
        EPS = 1e-06
        LN_EPS = 1e-05

        def _absmean_core(W):
            gamma = jnp.mean(jnp.abs(W)) + EPS
            Ws = W / gamma
            Wq = jnp.sign(Ws) * jnp.minimum(jnp.round(jnp.abs(Ws)), 1.0)
            return (Wq, gamma)

        @jax.custom_vjp
        def absmean(W):
            return _absmean_core(W)[0]

        def _absmean_fwd(W):
            Wq, gamma = _absmean_core(W)
            return (Wq, gamma)

        def _absmean_bwd(gamma, g):
            return (g / gamma,)
        absmean.defvjp(_absmean_fwd, _absmean_bwd)

        def layernorm(x, w, b, eps=LN_EPS):
            mu = jnp.mean(x, axis=-1, keepdims=True)
            var = jnp.mean((x - mu) ** 2, axis=-1, keepdims=True)
            return (x - mu) * jax.lax.rsqrt(var + eps) * w + b
        h = jnp.einsum('btd,hd->bth', x, absmean(W_fc))
        h = jax.nn.gelu(h, approximate=False)
        h = layernorm(h, ln_w, ln_b)
        return jnp.einsum('bth,dh->btd', h, absmean(W_proj))
    x = x + _L0_xattn_ref(_layernorm(x, axis=-1), ctx_1024, L0_xattn_w_sim, L0_xattn_b_sim, L0_xattn_W_qv, L0_xattn_b_qv)
    x = x + _L0_ffn_ref(_layernorm(x, axis=-1), L0_ffn_Win, L0_ffn_bin_, L0_ffn_W1, L0_ffn_b1, L0_ffn_W2, L0_ffn_b2, L0_ffn_Wout, L0_ffn_bout)
    x = x + _L1_xattn_ref(_layernorm(x, axis=-1), ctx_1024, ctx_1024, L1_xattn_WQ, L1_xattn_WK, L1_xattn_WV)
    x = x + _L1_ffn_ref(_layernorm(x, axis=-1), L1_ffn_W_fc, L1_ffn_ln_w, L1_ffn_ln_b, L1_ffn_W_proj)
    return x

_drawn_inputs = setup_inputs


def setup_inputs(seed=0):
    import zlib

    import numpy as np

    out = dict(_drawn_inputs(seed))
    spreads = {'L1_ffn_ln_w': (1.0, 0.2), 'L1_ffn_ln_b': (0.0, 0.1)}
    factors = {'L0_ffn_bin_': 8.0}
    for name, (base, spread) in spreads.items():
        noise = np.random.default_rng([zlib.crc32(name.encode()), seed]).standard_normal(out[name].shape)
        drawn = base * np.exp(spread * noise) if base else spread * noise
        out[name] = jnp.asarray(drawn.astype(out[name].dtype))
    for name, factor in factors.items():
        out[name] = (out[name] * factor).astype(out[name].dtype)
    return out
```

```python
from contextlib import ExitStack

import concourse.bass as bass
from concourse import mybir

P = 128
GT = 4
EPS = 1e-5
ABSMEAN_EPS = 1e-6

ALU = mybir.AluOpType
ACT = mybir.ActivationFunctionType
F32 = mybir.dt.float32
F16 = mybir.dt.float16
AX_X = mybir.AxisListType.X


def xattn_ffn_stack(nc, x, ctx, w_sim, b_sim, W_qv, b_qv, Win, bin_, W1, b1, W2, b2, Wout, bout,
                    WQ, WK, WV, W_fc, ln_w, ln_b, W_proj, out):
    NB, S, D = x.shape
    SK = ctx.shape[1]
    NG = NB // 2
    M, INNER = W1.shape
    HID = W_fc.shape[0]
    HC = HID // P
    assert D == P and S == 2 * P and SK == 64 and M == 64 and HC == 4
    GC = GT * P
    SCALE = float(D) ** -0.5
    RELU_PE = 8
    RING = 4

    with ExitStack() as es:
        def sb(name, shape, dt=F32):
            return es.enter_context(nc.sbuf_tensor(name, shape, dt))

        def sem(name):
            return es.enter_context(nc.semaphore(name))

        bank = [es.enter_context(nc.psum_tensor(f"bank{i}", [P, 512], F32)) for i in range(8)]

        X = sb("X", [P, NG * GC])
        CTX = sb("CTX", [P, NG * P])

        ident = sb("ident", [P, P])
        ones = sb("ones", [P, P])
        neg_half = sb("neg_half", [P, GT])
        eps = sb("eps", [P, GT])
        rows = sb("rows", [13, P])
        cols = sb("cols", [P, 13])
        w1_sim, w2_sim, w3_sim = cols[:, 0:1], cols[:, 1:2], cols[:, 2:3]
        lnw_col = [cols[:, 3 + c:4 + c] for c in range(HC)]
        lnb_col = [cols[:, 7 + c:8 + c] for c in range(HC)]
        b2_col, bin_col = cols[:, 11:12], cols[:, 12:13]
        w1_in = sb("w1_in", [P, INNER])
        b1_in = sb("b1_in", [P, INNER])
        w2_in = sb("w2_in", [P, INNER])
        wqv = sb("wqv", [P, 4, P])
        keys_bias = sb("keys_bias", [P, 2, P])
        bsim = sb("bsim", [P, 1])
        win = sb("win", [P, M])
        wout = sb("wout", [P, P])
        bout_rep = sb("bout_rep", [P, P])
        wq, wk, wv = sb("wq", [P, P]), sb("wk", [P, P]), sb("wv", [P, P])
        wfc = sb("wfc", [P, HC, P])
        wpj = sb("wpj", [P, HC, P])
        w2_rep = sb("w2_rep", [P, P])
        wkq = sb("wkq", [P, P])
        wvT = sb("wvT", [P, P])
        diag = sb("diag", [P, RELU_PE, P])
        absum = sb("absum", [P, 2])
        gamma = sb("gamma", [P, 2])
        inv_gamma = sb("inv_gamma", [P, 2])
        above = sb("above", [P, 2, HID])
        below = sb("below", [P, 2, HID])
        wfcT = sb("wfcT", [P, HID], F16)
        wpjT = sb("wpjT", [P, HC, P])
        wpjT_ln = sb("wpjT_ln", [P, HC, P])
        lnb_rep = sb("lnb_rep", [P, HC, P])
        out_bias = sb("out_bias", [P, P])

        def norm_set(c):
            return {"stats": sb(f"stats{c}", [P, GT, 6]), "mv": sb(f"mv{c}", [P, GT, 2]),
                    "ve": sb(f"ve{c}", [P, GT]), "rstd": sb(f"rstd{c}", [P, GT]),
                    "xn": sb(f"xn{c}", [P, GC])}

        nA, nB, nC, nD = norm_set("A"), norm_set("B"), norm_set("C"), norm_set("D")
        xTA, xTB, xTC = sb("xTA", [P, GC]), sb("xTB", [P, GC]), sb("xTC", [P, GC])
        ctxA, ctxC = sb("ctxA", [P, P]), sb("ctxC", [P, P])
        cTA, cTC = sb("cTA", [P, P]), sb("cTC", [P, P])
        simkey = sb("simkey", [P, P])
        keysA = sb("keysA", [P, 2, P])
        keysC = sb("keysC", [P, 2, P])
        simA = sb("simA", [P, 2, P])
        mxA, mxC = sb("mxA", [P, 4]), sb("mxC", [P, 4])
        shA, shC = sb("shA", [P, 2, P]), sb("shC", [P, 2, P])
        pA, pC = sb("pA", [P, 2, P]), sb("pC", [P, 2, P])
        smA, smC = sb("smA", [P, 4]), sb("smC", [P, 4])
        rsA, rsC = sb("rsA", [P, 4]), sb("rsC", [P, 4])
        aA, aC = sb("aA", [P, 2, P]), sb("aC", [P, 2, P])
        aTA, aTC = sb("aTA", [P, 2, P]), sb("aTC", [P, 2, P])
        m4 = sb("m4", [4, 1])
        m4d = sb("m4d", [4, 4])
        gmax = sb("gmax", [P, 2])
        msh = sb("msh", [P, 4])
        eb = sb("eb", [P, 4])
        esum = sb("esum", [P, 2])
        erec = sb("erec", [P, 2])
        hc = sb("hc", [P, 2])
        w14 = sb("w14", [P, 2, P])
        prodT = sb("prodT", [P, GC])
        sB = sb("sB", [P, 2 * P])
        uP = sb("uP", [P, RING, 2 * P])
        uV = sb("uV", [P, RING, 2 * P])
        accB = sb("accB", [P, 2 * P])
        gT = sb("gT", [P, 2 * P])
        xb = sb("xb", [P, GC])
        hiD = sb("hiD", [P, GC], F16)
        loD = sb("loD", [P, GC], F16)
        gel = sb("gel", [P, GT, HID])
        statsE = sb("statsE", [P, GT, 6])
        mvE = sb("mvE", [P, GT, 2])
        veE = sb("veE", [P, GT])
        rsE = sb("rsE", [P, GT])
        gn = sb("gn", [P, GT, HID])
        gnT = sb("gnT", [P, GT, HID])
        xe = sb("xe", [P, GC])

        ld_x = sem("ld_x")
        ld_ctx, ld_rows, ld_inner, ld_qv, ld_keys, ld_in, ld_out, ld_proj, ld_ffn = (
            sem(n) for n in ("ld_ctx", "ld_rows", "ld_inner", "ld_qv", "ld_keys", "ld_in", "ld_out",
                             "ld_proj", "ld_ffn"))
        stored = sem("stored")
        (s_ones, s_id0, s_ident, s_rowsT, s_cols, s_w2rep, s_bias, s_diag, s_wkq_mm, s_wkq, s_wvT_mm,
         s_wvT, s_absum, s_absum_mm, s_gamma, s_igamma, s_above, s_below, s_quant, s_fcT, s_fcT_cp, s_pjT, s_pjT_cp,
         s_lnb, s_ob, s_ob_cp, s_pjln) = (
            sem(n) for n in ("s_ones", "s_id0", "s_ident", "s_rowsT", "s_cols", "s_w2rep", "s_bias", "s_diag",
                             "s_wkq_mm", "s_wkq", "s_wvT_mm", "s_wvT", "s_absum", "s_absum_mm", "s_gamma", "s_igamma",
                             "s_above", "s_below", "s_quant", "s_fcT", "s_fcT_cp", "s_pjT", "s_pjT_cp",
                             "s_lnb", "s_ob", "s_ob_cp", "s_pjln"))

        def stage_sems(chain, names):
            return {n: sem(f"{chain}_{n}") for n in names.split()}

        NORM = "bn mv ve rstd xn xT_mm xT "
        A = stage_sems("A", NORM + "ctx cT_mm cT key keys_mm keys sim_mm sim mx sh p sm rs a aT_mm aT mxT_mm m4 m4d "
                 "gm_mm gmax msh eb hc_mm esum erec hc w14 hq_half hq_mm prod out_half out_mm x")
        B = stage_sems("B", NORM + "s_mm s uP uP_used uV acc gT xb out_half out_mm x")
        C = stage_sems("C", NORM + "ctx cT_mm cT keys_mm keys s_mm mx sh p sm rs a aT_mm aT out_half out_mm x")
        Dd = stage_sems("D", NORM + "lo fc_mm gel bn2 mv2")
        E = stage_sems("E", "ve rstd gn gT_mm gT xe out_mm x")

        block = es.enter_context(nc.Block())

        passed = {e: sem(f"passed_{e}") for e in ("sp", "dve", "pool")}

        def wait_alone(name, eng, semaphore, value):
            eng.wait_ge(semaphore, value)
            eng.sem_inc(passed[name], 1)

        def xg(g):
            return X[:, bass.ds(g * GC, GC)]

        def xtile(g, k):
            return X[:, bass.ds(g * GC + k * P, P)]

        def tiles(ap):
            return ap.rearrange("p (k d) -> p k d", k=GT)

        @block.sync
        def _(sp):
            def load_x(g):
                sp.dma_start(xg(g), x[bass.ds(2 * g, 2), :, :].rearrange("b (p t) d -> p b (t d)", t=2)).then_inc(ld_x, 16)
                wait_alone("sp", sp, ld_x, 16 * (g + 1))

            sp.dma_start(CTX[:, :].rearrange("k (g d) -> k g d", g=NG),
                         ctx.rearrange("(g b) k d -> (b k) g d", b=2)).then_inc(ld_ctx, 16)
            load_x(0)
            sp.dma_start(wqv[:, :, :], W_qv.rearrange("(k p) n -> p k n", p=P)).then_inc(ld_qv, 16)
            sp.dma_start(keys_bias[:, 0, :], b_qv.rearrange("(a n) -> a n", a=1).to_broadcast([P, P])).then_inc(ld_keys, 16)
            sp.dma_start(bsim[:, :], b_sim.rearrange("(a n) -> a n", a=1).to_broadcast([P, 1])).then_inc(ld_keys, 16)
            with sp.Fori(1, NG) as g:
                load_x(g)

            def store(g):
                wait_alone("sp", sp, E["x"], g + 1)
                sp.dma_start(out[bass.ds(2 * g, 2), :, :].rearrange("b (p t) d -> p b (t d)", t=2), xg(g)).then_inc(stored, 16)

            with sp.Fori(0, NG) as g:
                store(g)
            sp.wait_ge(stored, 16 * NG)

        @block.gpsimd
        def _(pool):
            pool.memset(ident[:, :], 0.0).then_inc(s_id0, 1)
            pool.wait_ge(s_id0, 1)
            pool.affine_select(out=ident[:, :], in_=ident[:, :], compare_op=ALU.not_equal, fill=1.0,
                               base=0, pattern=[[-1, P]], channel_multiplier=1).then_inc(s_ident, 1)
            pool.memset(ones[:, :], 1.0).then_inc(s_ones, 1)
            pool.memset(neg_half[:, :], -0.5).then_inc(s_ones, 1)
            pool.memset(eps[:, :], EPS).then_inc(s_ones, 1)
            for src, dst in ((Win, win[:, :]), (WQ, wq[:, :]), (WK, wk[:, :]), (WV, wv[:, :])):
                pool.dma_start(dst, src).then_inc(ld_in if dst.tensor is win else ld_proj, 16)
            for half in range(2):
                pool.dma_start(wout[half * M:(half + 1) * M, :], Wout).then_inc(ld_out, 16)
            pool.dma_start(bout_rep[:, :], bout.rearrange("(a n) -> a n", a=1).to_broadcast([P, P])).then_inc(ld_out, 16)
            pool.dma_start(wfc[:, :, :], W_fc.rearrange("(c p) d -> p c d", p=P)).then_inc(ld_ffn, 16)
            pool.dma_start(wpj[:, :, :], W_proj.rearrange("d (c h) -> d c h", c=HC)).then_inc(ld_ffn, 16)

            def rstd(ch, n, g):
                pool.wait_ge(ch["mv"], g + 1)
                pool.tensor_tensor(n["ve"][:, :], n["mv"][:, :, 1], eps[:, :], ALU.add).then_inc(ch["ve"], 1)
                pool.wait_ge(ch["ve"], g + 1)
                pool.tensor_tensor(n["rstd"][:, :], n["ve"][:, :], neg_half[:, :], ALU.pow).then_inc(ch["rstd"], 1)

            def context(ch, dst, g):
                pool.tensor_copy(dst[:, :], CTX[:, bass.ds(g * P, P)]).then_inc(ch["ctx"], 1)

            def sim_keys(g):
                wait_alone("pool", pool, A["cT"], g + 1)
                pool.tensor_scalar(simkey[:, :], cTA[:, :], w3_sim, w1_sim, ALU.mult, ALU.add).then_inc(A["key"], 1)

            def normalise(ch, p, rs, a, g):
                pool.wait_ge(ch["rs"], g + 1)
                pool.tensor_tensor(a[:, :, :].rearrange("p t (b j) -> p (t b) j", b=2),
                                   p[:, :, :].rearrange("p t (b j) -> p (t b) j", b=2),
                                   rs[:, :].unsqueeze(2).to_broadcast([P, 4, SK]), ALU.mult).then_inc(ch["a"], 1)

            def add_bout(g):
                pool.wait_ge(A["x"], g + 1)
                pool.tensor_tensor(tiles(xb[:, :]), tiles(xg(g)),
                                   bout_rep[:, :].unsqueeze(1).to_broadcast([P, GT, P]), ALU.add).then_inc(B["xb"], 1)

            pool.wait_ge(ld_ctx, 16)
            pool.wait_ge(s_ones, 3)
            pool.wait_ge(s_cols, 1)
            pool.wait_ge(ld_out, 48)

            def step(i, a, b, c):
                if a:
                    if not isinstance(i, int) or i >= 1:
                        pool.wait_ge(A["x"], i)
                    context(A, ctxA, i)
                if b:
                    rstd(B, nB, i - 1)
                if a:
                    rstd(A, nA, i)
                if c:
                    if not isinstance(i, int) or i >= 3:
                        pool.wait_ge(C["keys_mm"], i - 2)
                    context(C, ctxC, i - 2)
                    rstd(C, nC, i - 2)
                if a:
                    sim_keys(i)
                if b:
                    add_bout(i - 1)
                if a:
                    normalise(A, pA, rsA, aA, i)
                if c:
                    normalise(C, pC, rsC, aC, i - 2)

            step(0, True, False, False)
            step(1, True, True, False)
            with pool.Fori(2, NG) as i:
                step(i, True, True, True)
            step(NG, False, True, True)
            step(NG + 1, False, False, True)

            def add_out_bias(g):
                pool.wait_ge(C["x"], g + 1)
                if not isinstance(g, int) or g >= 1:
                    pool.wait_ge(E["x"], g)
                pool.tensor_tensor(tiles(xe[:, :]), tiles(xg(g)),
                                   out_bias[:, :].unsqueeze(1).to_broadcast([P, GT, P]), ALU.add).then_inc(E["xe"], 1)

            def rstd_hidden(g):
                pool.wait_ge(Dd["mv2"], GT * (g + 1))
                pool.tensor_tensor(veE[:, :], mvE[:, :, 1], eps[:, :], ALU.add).then_inc(E["ve"], 1)
                pool.wait_ge(E["ve"], g + 1)
                if not isinstance(g, int) or g >= 1:
                    pool.wait_ge(E["gn"], GT * g)
                pool.tensor_tensor(rsE[:, :], veE[:, :], neg_half[:, :], ALU.pow).then_inc(E["rstd"], 1)

            pool.wait_ge(s_ob_cp, 1)
            rstd(Dd, nD, 0)
            rstd(Dd, nD, 1)
            add_out_bias(0)
            rstd_hidden(0)
            with pool.Fori(1, NG - 1) as g:
                rstd(Dd, nD, g + 1)
                add_out_bias(g)
                rstd_hidden(g)
            add_out_bias(NG - 1)
            rstd_hidden(NG - 1)

        @block.scalar
        def _(act):
            act.dma_start(rows[0:3, :], w_sim.rearrange("(a n) -> a n", a=3)).then_inc(ld_rows, 16)
            act.dma_start(rows[3:7, :], ln_w.rearrange("(a n) -> a n", a=HC)).then_inc(ld_rows, 16)
            act.dma_start(rows[7:11, :], ln_b.rearrange("(a n) -> a n", a=HC)).then_inc(ld_rows, 16)
            for half in range(2):
                h0 = half * M
                act.dma_start(rows[11:12, h0:h0 + M], b2.rearrange("(a n) -> a n", a=1)).then_inc(ld_rows, 16)
                act.dma_start(rows[12:13, h0:h0 + M], bin_.rearrange("(a n) -> a n", a=1)).then_inc(ld_rows, 16)
                for src, dst in ((W1, w1_in), (b1, b1_in), (W2, w2_in)):
                    act.dma_start(dst[h0:h0 + M, :], src).then_inc(ld_inner, 16)
            act.wait_ge(s_rowsT, 1)
            act.activation(cols[:, :], bank[6][:, 0:13], ACT.Copy).then_inc(s_cols, 1)
            act.wait_ge(s_wkq_mm, 1)
            act.activation(wkq[:, :], bank[7][:, 0:P], ACT.Copy).then_inc(s_wkq, 1)
            act.wait_ge(s_wvT_mm, 1)
            act.activation(wvT[:, :], bank[7][:, P:2 * P], ACT.Copy).then_inc(s_wvT, 1)
            act.wait_ge(ld_inner, 96)
            act.wait_ge(s_cols, 1)

            def evac_xT(ch, src, dst, g):
                act.wait_ge(ch["xT_mm"], g + 1)
                act.activation(dst[:, :], src[:, :], ACT.Copy).then_inc(ch["xT"], 1)

            def evac_cT(ch, src, dst, g):
                act.wait_ge(ch["cT_mm"], g + 1)
                act.activation(dst[:, :], src[:, 0:P], ACT.Copy).then_inc(ch["cT"], 1)

            def exps(ch, sh, p, scale, g):
                act.wait_ge(ch["sh"], g + 1)
                act.activation(p[:, :, :], sh[:, :, :], ACT.Exp, scale=scale).then_inc(ch["p"], 1)

            def evac_aT(ch, src, dst, g):
                act.wait_ge(ch["aT_mm"], g + 1)
                act.activation(dst[:, :, :].rearrange("p t n -> p (t n)"), src[:, 0:2 * P], ACT.Copy).then_inc(ch["aT"], 1)

            def relus_pe(g, lo, hi):
                for h in range(lo, hi):
                    if h >= RING:
                        act.wait_ge(B["uP_used"], RELU_PE * g + h - RING + 1)
                    act.activation(uP[:, h % RING, :], sB[:, :], ACT.Relu, bias=b1_in[:, h:h + 1],
                                   scale=w1_in[:, h:h + 1]).then_inc(B["uP"], 1)

            def relus_dve(g, lo, hi):
                for h in range(lo, hi):
                    n = h - RELU_PE
                    if n >= RING:
                        act.wait_ge(B["acc"], (INNER - RELU_PE) * g + n - RING + 1)
                    act.activation(uV[:, n % RING, :], sB[:, :], ACT.Relu, bias=b1_in[:, h:h + 1],
                                   scale=w1_in[:, h:h + 1]).then_inc(B["uV"], 1)

            def step(i, a, b, c):
                if a:
                    evac_cT(A, bank[0], cTA, i)
                if b:
                    evac_xT(B, bank[5], xTB, i - 1)
                if c:
                    evac_cT(C, bank[1], cTC, i - 2)
                    act.wait_ge(C["keys_mm"], i - 1)
                    act.activation(keysC[:, :, :].rearrange("p a n -> p (a n)"), bank[1][:, 0:2 * P], ACT.Copy).then_inc(C["keys"], 1)
                if a:
                    evac_xT(A, bank[0], xTA, i)
                if b:
                    act.wait_ge(B["s_mm"], i)
                    act.activation(sB[:, :], bank[5][:, 0:2 * P], ACT.Identity, bias=bin_col).then_inc(B["s"], 1)
                    act.wait_ge(B["s"], i)
                    relus_pe(i - 1, 0, 2)
                if c:
                    evac_xT(C, bank[1], xTC, i - 2)
                if b:
                    relus_dve(i - 1, RELU_PE, RELU_PE + 2)
                if a:
                    exps(A, shA, pA, 1.0, i)
                if b:
                    relus_pe(i - 1, 2, 4)
                if a:
                    act.wait_ge(A["msh"], i + 1)
                    act.activation(eb[:, :], msh[:, :], ACT.Exp).then_inc(A["eb"], 1)
                if c:
                    exps(C, shC, pC, SCALE, i - 2)
                if b:
                    relus_dve(i - 1, RELU_PE + 2, RELU_PE + 4)
                if a:
                    evac_aT(A, bank[2], aTA, i)
                if b:
                    relus_pe(i - 1, 4, 6)
                if c:
                    evac_aT(C, bank[3], aTC, i - 2)
                if b:
                    relus_dve(i - 1, RELU_PE + 4, RELU_PE + 6)
                    relus_pe(i - 1, 6, RELU_PE)
                    relus_dve(i - 1, RELU_PE + 6, INNER)

            def transposed_weights():
                act.wait_ge(s_fcT, 1)
                act.activation(wfcT[:, :], bank[6][:, :], ACT.Copy).then_inc(s_fcT_cp, 1)
                act.wait_ge(s_pjT, 1)
                act.activation(wpjT[:, :, :].rearrange("p c d -> p (c d)"), bank[7][:, :], ACT.Copy).then_inc(s_pjT_cp, 1)
                act.wait_ge(s_ob, 1)
                act.activation(out_bias[:, :], bank[6][:, 0:P], ACT.Copy).then_inc(s_ob_cp, 1)

            step(0, True, False, False)
            transposed_weights()
            step(1, True, True, False)
            with act.Fori(2, NG) as i:
                step(i, True, True, True)
            step(NG, False, True, True)
            step(NG + 1, False, False, True)

            def high_half(g):
                act.wait_ge(Dd["xT_mm"], g + 1)
                if not isinstance(g, int) or g >= 1:
                    act.wait_ge(Dd["fc_mm"], GT * g)
                act.activation(hiD[:, :], bank[0][:, :], ACT.Copy).then_inc(Dd["xT"], 1)

            def gelu(g, k):
                act.wait_ge(Dd["fc_mm"], GT * g + k + 1)
                if not isinstance(g, int) or g >= 1:
                    act.wait_ge(E["gn"], GT * (g - 1) + k + 1)
                act.activation(gel[:, k, :], bank[1 + k % 2][:, :], ACT.Gelu).then_inc(Dd["gel"], 1)

            def evac_gT(g, k):
                act.wait_ge(E["gT_mm"], GT * g + k + 1)
                act.activation(gnT[:, k, :], bank[3 + k % 2][:, :], ACT.Copy).then_inc(E["gT"], 1)

            def step2(i, d, e):
                if d:
                    high_half(i)
                for k in range(GT):
                    if e:
                        evac_gT(i - 1, k)
                    if d:
                        gelu(i, k)

            step2(0, True, False)
            with act.Fori(1, NG) as i:
                step2(i, True, True)
            step2(NG, False, True)

        @block.vector
        def _(dve):
            def stats(ch, n, g):
                for k in range(GT):
                    dve.bn_stats(n["stats"][:, k, :], xtile(g, k)).then_inc(ch["bn"], 1)
                wait_alone("dve", dve, ch["bn"], GT * (g + 1))
                for k in range(GT):
                    last = dve.bn_aggr(n["mv"][:, k, :], n["stats"][:, k, :])
                last.then_inc(ch["mv"], 1)

            def norm(ch, n, g):
                dve.wait_ge(ch["rstd"], g + 1)
                for k in range(GT):
                    last = dve.tensor_scalar(n["xn"][:, k * P:(k + 1) * P], xtile(g, k), n["mv"][:, k, 0:1],
                                             n["rstd"][:, k:k + 1], ALU.subtract, ALU.mult)
                last.then_inc(ch["xn"], 1)

            def by_tile(ap):
                return ap.rearrange("p t (b j) -> p (t b) j", b=2)

            def softmax_front(ch, src, mx, sh, g):
                dve.tensor_reduce(mx[:, :], by_tile(src), AX_X, ALU.max).then_inc(ch["mx"], 1)
                dve.wait_ge(ch["mx"], g + 1)
                dve.tensor_tensor(by_tile(sh[:, :, :]), by_tile(src),
                                  mx[:, :].unsqueeze(2).to_broadcast([P, 4, SK]), ALU.subtract).then_inc(ch["sh"], 1)

            def softmax_back(ch, p, sm, rs, g):
                dve.wait_ge(ch["p"], g + 1)
                dve.tensor_reduce(sm[:, :], by_tile(p[:, :, :]), AX_X, ALU.add).then_inc(ch["sm"], 1)
                dve.wait_ge(ch["sm"], g + 1)
                dve.reciprocal(rs[:, :], sm[:, :]).then_inc(ch["rs"], 1)

            def accumulate(g, lo, hi):
                N = INNER - RELU_PE
                for n in range(lo, hi):
                    h = RELU_PE + n
                    dve.wait_ge(B["uV"], N * g + n + 1)
                    if n == 0:
                        dve.tensor_scalar(accB[:, :], uV[:, 0, :], w2_in[:, h:h + 1], b2_col,
                                          ALU.mult, ALU.add).then_inc(B["acc"], 1)
                    else:
                        dve.wait_ge(B["acc"], N * g + n)
                        dve.scalar_tensor_tensor(accB[:, :], uV[:, n % RING, :], w2_in[:, h:h + 1], accB[:, :],
                                                 ALU.mult, ALU.add).then_inc(B["acc"], 1)

            def batch_max(g):
                dve.wait_ge(A["mxT_mm"], g + 1)
                dve.tensor_reduce(m4[:, :], bank[4][0:4, 0:P], AX_X, ALU.max).then_inc(A["m4"], 1)
                dve.wait_ge(A["m4"], g + 1)
                dve.tensor_scalar(m4d[:, :], ident[0:4, 0:4], m4[:, 0:1], None, ALU.mult).then_inc(A["m4d"], 1)

            def batch_exp(g):
                dve.wait_ge(A["gm_mm"], g + 1)
                dve.tensor_reduce(gmax[:, :], bank[4][:, P:P + 4].rearrange("p (t b) -> p b t", b=2), AX_X,
                                  ALU.max).then_inc(A["gmax"], 1)
                dve.wait_ge(A["gmax"], g + 1)
                dve.tensor_tensor(msh[:, :].rearrange("p (t b) -> p t b", b=2), mxA[:, :].rearrange("p (t b) -> p t b", b=2),
                                  gmax[:, :].unsqueeze(1).to_broadcast([P, 2, 2]), ALU.subtract).then_inc(A["msh"], 1)

            def batch_mean(g):
                dve.wait_ge(A["hc_mm"], g + 1)
                dve.tensor_reduce(esum[:, :], bank[4][:, P + 4:P + 8].rearrange("p (t b) -> p b t", b=2), AX_X,
                                  ALU.add).then_inc(A["esum"], 1)
                dve.wait_ge(A["esum"], g + 1)
                dve.reciprocal(erec[:, :], esum[:, :]).then_inc(A["erec"], 1)
                dve.wait_ge(A["erec"], g + 1)
                dve.tensor_tensor(hc[:, :], bank[4][:, P + 8:P + 10], erec[:, :], ALU.mult).then_inc(A["hc"], 1)
                dve.wait_ge(A["hc"], g + 1)
                for b in range(2):
                    last = dve.scalar_tensor_tensor(w14[:, b, :], wqv[:, 3, :], hc[:, b:b + 1], wqv[:, 0, :],
                                                    ALU.mult, ALU.add)
                last.then_inc(A["w14"], 1)

            def residual(ch, src, g):
                dve.wait_ge(ch["out_mm"], g + 1)
                dve.tensor_tensor(xg(g), src[:, :], xg(g), ALU.add).then_inc(ch["x"], 1)
                wait_alone("dve", dve, ch["x"], g + 1)

            dve.wait_ge(s_cols, 1)
            dve.wait_ge(s_ones, 1)
            dve.tensor_scalar(w2_rep[:, :], ones[:, :], w2_sim, None, ALU.mult).then_inc(s_w2rep, 1)
            dve.wait_ge(ld_keys, 32)
            dve.tensor_scalar(keys_bias[:, 1, :], ones[:, :], bsim[:, 0:1], None, ALU.mult).then_inc(s_bias, 1)
            dve.wait_ge(s_bias, 1)
            dve.wait_ge(ld_qv, 16)
            dve.wait_ge(s_ident, 1)
            N = INNER - RELU_PE

            def step(i, a, b, c):
                if a:
                    wait_alone("dve", dve, ld_x, 16 * (i + 1))
                    stats(A, nA, i)
                if b:
                    norm(B, nB, i - 1)
                if c:
                    norm(C, nC, i - 2)
                if a:
                    norm(A, nA, i)
                    dve.wait_ge(A["keys_mm"], i + 1)
                    dve.tensor_tensor(keysA[:, :, :].rearrange("p a n -> p (a n)"), bank[0][:, P:3 * P],
                                      keys_bias[:, :, :].rearrange("p a n -> p (a n)"), ALU.add).then_inc(A["keys"], 1)
                    dve.wait_ge(A["sim_mm"], i + 1)
                    dve.wait_ge(A["keys"], i + 1)
                    dve.tensor_tensor(simA[:, :, :], bank[2][:, 0:2 * P].rearrange("p (t n) -> p t n", t=2),
                                      keysA[:, 1:2, :].to_broadcast([P, 2, P]), ALU.add).then_inc(A["sim"], 1)
                    dve.wait_ge(A["sim"], i + 1)
                    softmax_front(A, simA[:, :, :], mxA, shA, i)
                if b:
                    accumulate(i - 1, 0, 1)
                if c:
                    dve.wait_ge(C["s_mm"], i - 1)
                    softmax_front(C, bank[3][:, 0:2 * P].rearrange("p (t n) -> p t n", t=2), mxC, shC, i - 2)
                if a:
                    batch_max(i)
                    softmax_back(A, pA, smA, rsA, i)
                    batch_exp(i)
                if b:
                    accumulate(i - 1, 1, 2)
                if c:
                    softmax_back(C, pC, smC, rsC, i - 2)
                if b:
                    accumulate(i - 1, 2, 3)
                if a:
                    batch_mean(i)
                if b:
                    accumulate(i - 1, 3, 5)
                if a:
                    dve.wait_ge(A["hq_mm"], i + 1)
                    dve.tensor_tensor(prodT[:, :], bank[4][:, :], xTA[:, :], ALU.mult).then_inc(A["prod"], 1)
                if b:
                    accumulate(i - 1, 5, 7)
                if c:
                    residual(C, bank[6], i - 2)
                if b:
                    accumulate(i - 1, 7, N)
                    dve.wait_ge(B["uP_used"], RELU_PE * i)
                    dve.wait_ge(B["acc"], N * i)
                    dve.tensor_tensor(gT[:, :], bank[5][:, 0:2 * P], accB[:, :], ALU.add).then_inc(B["gT"], 1)
                if a:
                    residual(A, bank[7], i)
                    stats(B, nB, i)
                if b:
                    dve.wait_ge(B["out_mm"], i)
                    dve.wait_ge(B["xb"], i)
                    dve.tensor_tensor(xg(i - 1), bank[6][:, :], xb[:, :], ALU.add).then_inc(B["x"], 1)
                    wait_alone("dve", dve, B["x"], i)
                    stats(C, nC, i - 1)

            def quantise():
                dve.wait_ge(ld_ffn, 32)
                for k, w in enumerate((wfc, wpj)):
                    dve.tensor_reduce(absum[:, k:k + 1], w[:, :, :].rearrange("p c d -> p (c d)"), AX_X, ALU.add,
                                      apply_absolute_value=True).then_inc(s_absum, 1)
                dve.wait_ge(s_absum_mm, 1)
                dve.tensor_scalar(gamma[:, :], bank[6][:, 16:18], 1.0 / (HID * D), ABSMEAN_EPS, ALU.mult, ALU.add).then_inc(s_gamma, 1)
                dve.wait_ge(s_gamma, 1)
                dve.reciprocal(inv_gamma[:, :], gamma[:, :]).then_inc(s_igamma, 1)
                dve.wait_ge(s_igamma, 1)
                for k, w in enumerate((wfc, wpj)):
                    flat = w[:, :, :].rearrange("p c d -> p (c d)")
                    dve.tensor_scalar(above[:, k, :], flat, inv_gamma[:, k:k + 1], 0.5, ALU.mult, ALU.is_gt).then_inc(s_above, 1)
                    dve.tensor_scalar(below[:, k, :], flat, inv_gamma[:, k:k + 1], -0.5, ALU.mult, ALU.is_lt).then_inc(s_above, 1)
                    dve.wait_ge(s_above, 2 * (k + 1))
                    dve.tensor_tensor(flat, above[:, k, :], below[:, k, :], ALU.subtract).then_inc(s_quant, 1)
                for c in range(HC):
                    dve.tensor_scalar(lnb_rep[:, c, :], ones[:, :], lnb_col[c], None, ALU.mult).then_inc(s_lnb, 1)
                dve.wait_ge(s_pjT_cp, 1)
                for c in range(HC):
                    dve.tensor_scalar(wpjT_ln[:, c, :], wpjT[:, c, :], lnw_col[c], None, ALU.mult).then_inc(s_pjln, 1)

            def diagonals():
                dve.wait_ge(ld_inner, 96)
                for h in range(RELU_PE):
                    dve.tensor_scalar(diag[:, h, :], ident[:, :], w2_in[:, h:h + 1], None, ALU.mult).then_inc(s_diag, 1)

            step(0, True, False, False)
            diagonals()
            quantise()
            step(1, True, True, False)
            with dve.Fori(2, NG) as i:
                step(i, True, True, True)
            step(NG, False, True, True)
            step(NG + 1, False, False, True)

            def low_half(g):
                dve.wait_ge(Dd["xT"], g + 1)
                dve.tensor_tensor(loD[:, :], bank[0][:, :], hiD[:, :], ALU.subtract).then_inc(Dd["lo"], 1)

            def hidden_stats(g, k):
                wait_alone("dve", dve, Dd["gel"], GT * g + k + 1)
                dve.bn_stats(statsE[:, k, :], gel[:, k, :]).then_inc(Dd["bn2"], 1)

            def hidden_aggr(g):
                wait_alone("dve", dve, Dd["bn2"], GT * (g + 1))
                for k in range(GT):
                    dve.bn_aggr(mvE[:, k, :], statsE[:, k, :]).then_inc(Dd["mv2"], 1)

            def hidden_norm(g, k):
                dve.tensor_scalar(gn[:, k, :], gel[:, k, :], mvE[:, k, 0:1], rsE[:, k:k + 1],
                                  ALU.subtract, ALU.mult).then_inc(E["gn"], 1)

            def step2(i, d, e):
                if e:
                    dve.wait_ge(E["rstd"], i)
                    for k in range(GT):
                        hidden_norm(i - 1, k)
                if d:
                    low_half(i)
                    for k in range(GT):
                        hidden_stats(i, k)
                    hidden_aggr(i)
                if e:
                    dve.wait_ge(E["out_mm"], i)
                    dve.wait_ge(E["xe"], i)
                    dve.tensor_tensor(xg(i - 1), bank[5][:, :], xe[:, :], ALU.add).then_inc(E["x"], 1)

            stats(Dd, nD, 0)
            norm(Dd, nD, 0)
            step2(0, True, False)
            stats(Dd, nD, 1)
            norm(Dd, nD, 1)
            with dve.Fori(1, NG - 1) as i:
                step2(i, True, True)
                stats(Dd, nD, i + 1)
                norm(Dd, nD, i + 1)
            step2(NG - 1, True, True)
            step2(NG, False, True)

        @block.tensor
        def _(pe):
            def xT(ch, n, dst, g):
                pe.wait_ge(ch["xn"], g + 1)
                for k in range(GT):
                    last = pe.transpose(dst[:, k * P:(k + 1) * P], n["xn"][:, k * P:(k + 1) * P], ident[:, :])
                last.then_inc(ch["xT_mm"], 1)

            def cT(ch, src, dst, g):
                pe.wait_ge(ch["ctx"], g + 1)
                pe.transpose(dst[:, 0:P], src[:, :], ident[:, :]).then_inc(ch["cT_mm"], 1)

            def scores(ch, done, xt, keys, dst, g):
                for t in range(2):
                    for b in range(2):
                        k = 2 * b + t
                        last = pe.matmul(dst[:, t * P + b * SK:t * P + (b + 1) * SK], xt[:, k * P:(k + 1) * P],
                                         keys[:, b * SK:(b + 1) * SK], start=True, stop=True)
                last.then_inc(done, 1)

            def aT(ch, a, dst, g):
                pe.wait_ge(ch["a"], g + 1)
                for t in range(2):
                    last = pe.transpose(dst[:, t * P:(t + 1) * P], a[:, t, :], ident[:, :])
                last.then_inc(ch["aT_mm"], 1)

            def sum_units(g, lo, hi):
                for h in range(lo, hi):
                    pe.wait_ge(B["uP"], RELU_PE * g + h + 1)
                    mm = pe.matmul(bank[5][:, 0:2 * P], diag[:, h, :], uP[:, h % RING, :], start=(h == 0),
                                   stop=(h == RELU_PE - 1))
                    mm.then_inc(B["uP_used"], 1)

            def outA(g):
                pe.wait_ge(A["w14"], g + 1)
                pe.wait_ge(A["prod"], g + 1)
                for b in range(2):
                    rows_b = slice(b * SK, (b + 1) * SK)
                    for t in range(2):
                        k = 2 * b + t
                        o = bank[7][:, k * P:(k + 1) * P]
                        pe.matmul(o, aTA[rows_b, t, :], keysA[rows_b, 0, :], start=True, stop=False)
                        pe.matmul(o, xTA[:, k * P:(k + 1) * P], w14[:, b, :], start=False, stop=False)
                        last = pe.matmul(o, prodT[:, k * P:(k + 1) * P], wqv[:, 2, :], start=False, stop=True)
                    if b == 0:
                        last.then_inc(A["out_half"], 1)
                        pe.wait_ge(A["out_half"], g + 1)
                last.then_inc(A["out_mm"], 1)

            def outB(g):
                pe.wait_ge(B["gT"], g + 1)
                for b in range(2):
                    rows_b = slice(b * M, (b + 1) * M)
                    for t in range(2):
                        k = 2 * b + t
                        last = pe.matmul(bank[6][:, k * P:(k + 1) * P], gT[rows_b, t * P:(t + 1) * P], wout[rows_b, :],
                                         start=True, stop=True)
                    if b == 0:
                        last.then_inc(B["out_half"], 1)
                        pe.wait_ge(B["out_half"], g + 1)
                last.then_inc(B["out_mm"], 1)

            def outC(g):
                pe.wait_ge(C["aT"], g + 1)
                pe.wait_ge(B["x"], g + 1)
                for b in range(2):
                    rows_b = slice(b * SK, (b + 1) * SK)
                    for t in range(2):
                        k = 2 * b + t
                        last = pe.matmul(bank[6][:, k * P:(k + 1) * P], aTC[rows_b, t, :], keysC[rows_b, 1, :],
                                         start=True, stop=True)
                    if b == 0:
                        last.then_inc(C["out_half"], 1)
                        pe.wait_ge(C["out_half"], g + 1)
                last.then_inc(C["out_mm"], 1)

            pe.wait_ge(s_ident, 1)
            pe.wait_ge(ld_rows, 112)
            pe.transpose(bank[6][:, 0:13], rows[:, :], ident[0:13, 0:13]).then_inc(s_rowsT, 1)
            pe.wait_ge(ld_proj, 48)
            pe.matmul(bank[7][:, 0:P], wk[:, :], wq[:, :], start=True, stop=True).then_inc(s_wkq_mm, 1)
            pe.wait_ge(s_wkq, 1)
            pe.transpose(bank[7][:, P:2 * P], wv[:, :], ident[:, :]).then_inc(s_wvT_mm, 1)
            pe.wait_ge(s_wvT, 1)
            pe.wait_ge(s_w2rep, 1)
            pe.wait_ge(ld_qv, 16)
            pe.wait_ge(ld_in, 16)
            pe.wait_ge(ld_out, 48)
            pe.wait_ge(s_ones, 1)

            def step(i, a, b, c):
                if a:
                    cT(A, ctxA, bank[0], i)
                if b:
                    xT(B, nB, bank[5], i - 1)
                if c:
                    cT(C, ctxC, bank[1], i - 2)
                if a:
                    pe.wait_ge(A["cT"], i + 1)
                    pe.matmul(bank[0][:, P:2 * P], cTA[:, :], wqv[:, 1, :], start=True, stop=True)
                    pe.matmul(bank[0][:, 2 * P:3 * P], w2_rep[:, :], cTA[:, :], start=True, stop=True).then_inc(A["keys_mm"], 1)
                if c:
                    pe.wait_ge(C["cT"], i - 1)
                    pe.matmul(bank[1][:, 0:P], wkq[:, :], cTC[:, :], start=True, stop=True)
                    pe.matmul(bank[1][:, P:2 * P], cTC[:, :], wvT[:, :], start=True, stop=True).then_inc(C["keys_mm"], 1)
                if b:
                    pe.wait_ge(B["xT"], i)
                    for half in range(2):
                        last = pe.matmul(bank[5][half * M:(half + 1) * M, 0:2 * P], win[:, :],
                                         xTB[:, half * 2 * P:(half + 1) * 2 * P], start=True, stop=True)
                    last.then_inc(B["s_mm"], 1)
                if a:
                    pe.wait_ge(A["keys"], i + 1)
                    xT(A, nA, bank[0], i)
                if c:
                    pe.wait_ge(C["keys"], i - 1)
                    xT(C, nC, bank[1], i - 2)
                if a:
                    pe.wait_ge(A["xT"], i + 1)
                    pe.wait_ge(A["key"], i + 1)
                    scores(A, A["sim_mm"], xTA, simkey, bank[2], i)
                if b:
                    if isinstance(i, int) and i == 1:
                        pe.wait_ge(s_diag, RELU_PE)
                    sum_units(i - 1, 0, 2)
                if c:
                    pe.wait_ge(C["xT"], i - 1)
                    scores(C, C["s_mm"], xTC, keysC[:, 0, :], bank[3], i - 2)
                if a:
                    pe.wait_ge(A["mx"], i + 1)
                    pe.transpose(bank[4][0:4, 0:P], mxA[:, :], ident[:, :]).then_inc(A["mxT_mm"], 1)
                if b:
                    sum_units(i - 1, 2, 3)
                if a:
                    pe.wait_ge(A["m4d"], i + 1)
                    pe.matmul(bank[4][:, P:P + 4], ones[0:4, :], m4d[:, :], start=True, stop=True).then_inc(A["gm_mm"], 1)
                if b:
                    sum_units(i - 1, 3, 4)
                if a:
                    aT(A, aA, bank[2], i)
                    pe.wait_ge(A["eb"], i + 1)
                    pe.matmul(bank[4][:, P + 4:P + 8], ones[:, :], eb[:, :], start=True, stop=True)
                    for b_ in range(2):
                        for t in range(2):
                            k = 2 * b_ + t
                            last = pe.matmul(bank[4][:, P + 8 + b_:P + 9 + b_], nA["xn"][:, k * P:(k + 1) * P],
                                             eb[:, 2 * t + b_:2 * t + b_ + 1], start=(t == 0), stop=(t == 1))
                    last.then_inc(A["hc_mm"], 1)
                if b:
                    sum_units(i - 1, 4, 5)
                if c:
                    aT(C, aC, bank[3], i - 2)
                if a:
                    pe.wait_ge(A["aT"], i + 1)
                    pe.wait_ge(A["hc"], i + 1)
                    for b_ in range(2):
                        rows_b = slice(b_ * SK, (b_ + 1) * SK)
                        last = pe.matmul(bank[4][:, b_ * 2 * P:(b_ + 1) * 2 * P], ctxA[rows_b, :],
                                         aTA[rows_b, :, :].rearrange("p t n -> p (t n)"), start=True, stop=True)
                        if b_ == 0:
                            last.then_inc(A["hq_half"], 1)
                            pe.wait_ge(A["hq_half"], i + 1)
                    last.then_inc(A["hq_mm"], 1)
                if b:
                    sum_units(i - 1, 5, 7)
                if c:
                    outC(i - 2)
                if b:
                    sum_units(i - 1, 7, RELU_PE)
                if a:
                    outA(i)
                if b:
                    if c:
                        pe.wait_ge(C["x"], i - 1)
                    outB(i - 1)

            def quantised():
                pe.wait_ge(s_absum, 2)
                pe.matmul(bank[6][:, 16:18], ones[:, :], absum[:, :], start=True, stop=True).then_inc(s_absum_mm, 1)
                pe.wait_ge(s_quant, 1)
                for c in range(HC):
                    last = pe.transpose(bank[6][:, c * P:(c + 1) * P], wfc[:, c, :], ident[:, :])
                last.then_inc(s_fcT, 1)
                pe.wait_ge(s_quant, 2)
                pe.wait_ge(A["x"], 1)
                for c in range(HC):
                    last = pe.transpose(bank[7][:, c * P:(c + 1) * P], wpj[:, c, :], ident[:, :])
                last.then_inc(s_pjT, 1)
                pe.wait_ge(s_pjT_cp, 1)
                pe.wait_ge(s_fcT_cp, 1)
                pe.wait_ge(s_lnb, HC)
                for c in range(HC):
                    last = pe.matmul(bank[6][:, 0:P], lnb_rep[:, c, :], wpjT[:, c, :], start=(c == 0), stop=(c == HC - 1))
                last.then_inc(s_ob, 1)
                pe.wait_ge(s_ob_cp, 1)

            step(0, True, False, False)
            quantised()
            step(1, True, True, False)
            with pe.Fori(2, NG) as i:
                step(i, True, True, True)
            step(NG, False, True, True)
            step(NG + 1, False, False, True)

            def up(g, k):
                n = GT * g + k
                if k >= 2 or not isinstance(g, int) or g >= 1:
                    pe.wait_ge(Dd["gel"], n - 1)
                o = bank[1 + k % 2][:, :]
                pe.matmul(o, hiD[:, k * P:(k + 1) * P], wfcT[:, :], start=True, stop=False)
                pe.matmul(o, loD[:, k * P:(k + 1) * P], wfcT[:, :], start=False, stop=True).then_inc(Dd["fc_mm"], 1)

            def turn(g, k):
                n = GT * g + k
                pe.wait_ge(E["gn"], n + 1)
                if k >= 2 or not isinstance(g, int) or g >= 1:
                    pe.wait_ge(E["gT"], n - 1)
                for c in range(HC):
                    last = pe.transpose(bank[3 + k % 2][:, c * P:(c + 1) * P], gn[:, k, c * P:(c + 1) * P], ident[:, :])
                last.then_inc(E["gT_mm"], 1)

            def down(g, k):
                pe.wait_ge(E["gT"], GT * g + k + 1)
                if k == 0 and (not isinstance(g, int) or g >= 1):
                    pe.wait_ge(E["x"], g)
                for c in range(HC):
                    last = pe.matmul(bank[5][:, k * P:(k + 1) * P], gnT[:, k, c * P:(c + 1) * P], wpjT_ln[:, c, :],
                                     start=(c == 0), stop=(c == HC - 1))
                if k == GT - 1:
                    last.then_inc(E["out_mm"], 1)

            def step2(i, d, e):
                if d:
                    if not isinstance(i, int) or i >= 1:
                        pe.wait_ge(Dd["lo"], i)
                    xT(Dd, nD, bank[0], i)
                for k in range(GT):
                    if e:
                        turn(i - 1, k)
                    if d:
                        if k == 0:
                            pe.wait_ge(Dd["lo"], i + 1)
                        up(i, k)
                    if e and k >= 1:
                        down(i - 1, k - 1)
                if e:
                    down(i - 1, GT - 1)

            pe.wait_ge(s_pjln, HC)
            step2(0, True, False)
            step2(1, True, True)
            with pe.Fori(2, NG) as i:
                step2(i, True, True)
            step2(NG, False, True)


_INS = ["x", "ctx_1024", "L0_xattn_w_sim", "L0_xattn_b_sim", "L0_xattn_W_qv", "L0_xattn_b_qv", "L0_ffn_Win",
        "L0_ffn_bin_", "L0_ffn_W1", "L0_ffn_b1", "L0_ffn_W2", "L0_ffn_b2", "L0_ffn_Wout", "L0_ffn_bout",
        "L1_xattn_WQ", "L1_xattn_WK", "L1_xattn_WV", "L1_ffn_W_fc", "L1_ffn_ln_w", "L1_ffn_ln_b",
        "L1_ffn_W_proj"]


def kernel(**inputs):
    import numpy as np
    import concourse.bacc as bacc
    from concourse.bass_utils import run_bass_kernel_spmd

    nc = bacc.Bacc("TRN2", target_bir_lowering=False, num_devices=1)
    arrays, args = {}, []
    for name in _INS:
        a = np.ascontiguousarray(inputs[name])
        arrays[f"in_{name}"] = a
        args.append(nc.dram_tensor(f"in_{name}", a.shape, mybir.dt.from_np(a.dtype), kind="ExternalInput").ap())
    shape = inputs["x"].shape
    out = nc.dram_tensor("out_0", shape, F32, kind="ExternalOutput").ap()
    xattn_ffn_stack(nc, *args, out)
    r = run_bass_kernel_spmd(nc, [arrays], core_ids=[0])
    return r.results[0]["out_0"]
```

```python
from contextlib import ExitStack

import concourse.bass as bass
from concourse import mybir

P = 128
GT = 4
EPS = 1e-5
ABSMEAN_EPS = 1e-6

ALU = mybir.AluOpType
ACT = mybir.ActivationFunctionType
F32 = mybir.dt.float32
F16 = mybir.dt.float16
AX_X = mybir.AxisListType.X


def xattn_ffn_stack(nc, x, ctx, w_sim, b_sim, W_qv, b_qv, Win, bin_, W1, b1, W2, b2, Wout, bout,
                    WQ, WK, WV, W_fc, ln_w, ln_b, W_proj, out):
    NB, S, D = x.shape
    SK = ctx.shape[1]
    NG = NB // 2
    M, INNER = W1.shape
    HID = W_fc.shape[0]
    HC = HID // P
    assert D == P and S == 2 * P and SK == 64 and M == 64 and HC == 4
    GC = GT * P
    SCALE = float(D) ** -0.5
    HALF = INNER // 2
    KP = 4
    KV = HALF - KP
    K = 3

    with ExitStack() as es:
        def sb(name, shape, dt=F32):
            return es.enter_context(nc.sbuf_tensor(name, shape, dt))

        def sem(name):
            return es.enter_context(nc.semaphore(name))

        bank = [es.enter_context(nc.psum_tensor(f"bank{i}", [P, 512], F32)) for i in range(8)]

        X = sb("X", [P, NG * GC])
        CTX = sb("CTX", [P, NG * P])

        ident = sb("ident", [P, P])
        ones = sb("ones", [P, P])
        neg_half = sb("neg_half", [P, GT])
        eps = sb("eps", [P, GT])
        rows = sb("rows", [13, P])
        cols = sb("cols", [P, 13])
        w1_sim, w2_sim, w3_sim = cols[:, 0:1], cols[:, 1:2], cols[:, 2:3]
        lnw_col = [cols[:, 3 + c:4 + c] for c in range(HC)]
        lnb_col = [cols[:, 7 + c:8 + c] for c in range(HC)]
        b2_col, bin_col = cols[:, 11:12], cols[:, 12:13]
        w1_in = sb("w1_in", [P, HALF])
        b1_in = sb("b1_in", [P, HALF])
        w2_in = sb("w2_in", [P, HALF])
        b1_s = sb("b1_s", [P, HALF])
        b2_half = sb("b2_half", [P, 1])
        wqv = sb("wqv", [P, 4, P])
        bqv_rep = sb("bqv_rep", [P, P])
        bsim = sb("bsim", [P, 1])
        win = sb("win", [P, 2, M])
        wout = sb("wout", [P, P])
        bout_rep = sb("bout_rep", [P, P])
        wq, wk, wv = sb("wq", [P, P]), sb("wk", [P, P]), sb("wv", [P, P])
        wfc = sb("wfc", [P, HC, P])
        wpj = sb("wpj", [P, HC, P])
        w2_rep = sb("w2_rep", [P, P])
        wkq = sb("wkq", [P, P])
        wvT = sb("wvT", [P, P])
        wsum = sb("wsum", [P, KP, P])
        cT = sb("cT", [P, NG * P])
        simkey = sb("simkey", [P, NG * P])
        rkey = sb("rkey", [P, NG * P])
        cw2 = sb("cw2", [P, NG * P])
        projkey = sb("projkey", [P, NG * P])
        values = sb("values", [P, NG * P])
        absum = sb("absum", [P, 2])
        gamma = sb("gamma", [P, 2])
        inv_gamma = sb("inv_gamma", [P, 2])
        above = sb("above", [P, 2, HID])
        below = sb("below", [P, 2, HID])
        wfcT = sb("wfcT", [P, HID], F16)
        wpjT = sb("wpjT", [P, HC, P])
        wpjT_ln = sb("wpjT_ln", [P, HC, P])
        lnb_rep = sb("lnb_rep", [P, HC, P])
        out_bias = sb("out_bias", [P, P])

        def norm_set(c):
            return {"stats": sb(f"stats{c}", [P, GT, 6]), "mv": sb(f"mv{c}", [P, GT, 2]),
                    "ve": sb(f"ve{c}", [P, GT]), "rstd": sb(f"rstd{c}", [P, GT]),
                    "xn": sb(f"xn{c}", [P, GC])}

        nA, nB, nC, nD = norm_set("A"), norm_set("B"), norm_set("C"), norm_set("D")
        xTA, xTB, xTC = sb("xTA", [P, GC]), sb("xTB", [P, GC]), sb("xTC", [P, GC])
        ctxA = sb("ctxA", [P, P])
        simA = sb("simA", [P, 2, P])
        mxA, mxC = sb("mxA", [P, 4]), sb("mxC", [P, 4])
        pA, pC = sb("pA", [P, 2, P]), sb("pC", [P, 2, P])
        smA, smC = sb("smA", [P, 4]), sb("smC", [P, 4])
        rsA, rsC = sb("rsA", [P, 4]), sb("rsC", [P, 4])
        aA, aC = sb("aA", [P, 2, P]), sb("aC", [P, 2, P])
        aTA, aTC = sb("aTA", [P, 2, 2 * P]), sb("aTC", [P, 2, 2 * P])
        m4 = sb("m4", [4, 1])
        m4d = sb("m4d", [4, 4])
        gmax = sb("gmax", [P, 2])
        msh = sb("msh", [P, 4])
        eb = sb("eb", [P, 4])
        erec = sb("erec", [P, 2])
        hc = sb("hc", [P, 2])
        w14 = sb("w14", [P, 2, P])
        prodT = sb("prodT", [P, GC])
        u = sb("u", [P, HALF, GC])
        acc = sb("acc", [P, GC])
        xb = sb("xb", [P, GC])
        hiD = sb("hiD", [P, GC], F16)
        loD = sb("loD", [P, GC], F16)
        gel = sb("gel", [P, GT, HID])
        statsE = sb("statsE", [P, GT, 6])
        mvE = sb("mvE", [P, GT, 2])
        veE = sb("veE", [P, GT])
        rsE = sb("rsE", [P, GT])
        gn = sb("gn", [P, GT, HID])
        gnT = sb("gnT", [P, GT, HID])
        xe = sb("xe", [P, GC])

        scoresC = bank[3][:, 0:2 * P].rearrange("p (t n) -> p t n", t=2)

        ld_x = sem("ld_x")
        ld_ctx, ld_rows, ld_inner, ld_qv, ld_keys, ld_in, ld_out, ld_proj, ld_ffn = (
            sem(n) for n in ("ld_ctx", "ld_rows", "ld_inner", "ld_qv", "ld_keys", "ld_in", "ld_out",
                             "ld_proj", "ld_ffn"))
        stored = sem("stored")
        (s_zero, s_ones, s_id0, s_ident, s_rows0, s_rowsT, s_cols, s_w2rep, s_b1, s_b1s, s_wsum, s_wk_mm, s_wk,
         s_cT_mm, s_cT, s_simkey, s_keys_mm, s_rkey, s_cw2, s_pv_mm, s_pv,
         s_absum, s_absum_mm, s_gamma, s_igamma, s_above, s_quant, s_fcT, s_fcT_cp, s_pjT, s_pjT_cp,
         s_lnb, s_ob, s_ob_cp, s_pjln) = (
            sem(n) for n in ("s_zero", "s_ones", "s_id0", "s_ident", "s_rows0", "s_rowsT", "s_cols", "s_w2rep",
                             "s_b1", "s_b1s", "s_wsum", "s_wk_mm", "s_wk", "s_cT_mm", "s_cT", "s_simkey", "s_keys_mm",
                             "s_rkey", "s_cw2", "s_pv_mm", "s_pv",
                             "s_absum", "s_absum_mm", "s_gamma", "s_igamma", "s_above", "s_quant", "s_fcT",
                             "s_fcT_cp", "s_pjT", "s_pjT_cp", "s_lnb", "s_ob", "s_ob_cp", "s_pjln"))

        def stage_sems(chain, names):
            return {n: sem(f"{chain}_{n}") for n in names.split()}

        NORM = "bn mv ve rstd xn xT_mm xT "
        A = stage_sems("A", NORM + "ctx s_mm sim mx p rs a aT_mm aT mxT_mm m4 m4d gm_mm gmax msh eb hc_mm erec hc "
                       "w14 hq_mm prod out_mm x")
        B = stage_sems("B", NORM + "s_mm uP uV sum acc xb out_mm x")
        C = stage_sems("C", NORM + "s_mm mx p rs a aT_mm aT out_mm x")
        Dd = stage_sems("D", NORM + "lo fc_mm gel bn2 mv2")
        E = stage_sems("E", "ve rstd gn gT_mm gT xe out_mm x")

        block = es.enter_context(nc.Block())

        passed = {e: sem(f"passed_{e}") for e in ("sp", "dve", "pool")}

        def wait_alone(name, eng, semaphore, value):
            eng.wait_ge(semaphore, value)
            eng.sem_inc(passed[name], 1)

        def at_step(i):
            return lambda behind: not isinstance(i, int) or 0 <= i - behind < NG

        def before(eng, semaphore, g, per_group=1, n=0):
            if not isinstance(g, int) or g >= 1:
                eng.wait_ge(semaphore, per_group * g + n)

        def xg(g):
            return X[:, bass.ds(g * GC, GC)]

        def keys_of(t, g):
            return t[:, bass.ds(g * P, P)]

        def xtile(g, k):
            return X[:, bass.ds(g * GC + k * P, P)]

        def tiles(ap):
            return ap.rearrange("p (k d) -> p k d", k=GT)

        @block.sync
        def _(sp):
            def load_x(g):
                sp.dma_start(xg(g), x[bass.ds(2 * g, 2), :, :].rearrange("b (p t) d -> p b (t d)", t=2)).then_inc(ld_x, 16)
                wait_alone("sp", sp, ld_x, 16 * (g + 1))

            sp.dma_start(CTX[:, :].rearrange("k (g d) -> k g d", g=NG),
                         ctx.rearrange("(g b) k d -> (b k) g d", b=2)).then_inc(ld_ctx, 16)
            load_x(0)
            def load_keys(g):
                before(sp, A["hq_mm"], g)
                sp.dma_start(ctxA[:, :], ctx[bass.ds(2 * g, 2), :, :].rearrange("b k d -> (b k) d")).then_inc(A["ctx"], 16)

            sp.dma_start(wqv[:, :, :], W_qv.rearrange("(k p) n -> p k n", p=P)).then_inc(ld_qv, 16)
            sp.dma_start(bqv_rep[:, :], b_qv.rearrange("(a n) -> a n", a=1).to_broadcast([P, P])).then_inc(ld_keys, 16)
            sp.dma_start(bsim[:, :], b_sim.rearrange("(a n) -> a n", a=1).to_broadcast([P, 1])).then_inc(ld_keys, 16)
            load_keys(0)
            with sp.Fori(1, NG) as g:
                load_x(g)
            with sp.Fori(1, NG) as g:
                load_keys(g)

            def store(g):
                wait_alone("sp", sp, E["x"], g + 1)
                sp.dma_start(out[bass.ds(2 * g, 2), :, :].rearrange("b (p t) d -> p b (t d)", t=2), xg(g)).then_inc(stored, 16)

            with sp.Fori(0, NG) as g:
                store(g)
            sp.wait_ge(stored, 16 * NG)

        @block.gpsimd
        def _(pool):
            pool.memset(rows[:, :], 0.0).then_inc(s_rows0, 1)
            pool.memset(ident[:, :], 0.0).then_inc(s_id0, 1)
            pool.wait_ge(s_id0, 1)
            pool.affine_select(out=ident[:, :], in_=ident[:, :], compare_op=ALU.not_equal, fill=1.0,
                               base=0, pattern=[[-1, P]], channel_multiplier=1).then_inc(s_ident, 1)
            pool.memset(ones[:, :], 1.0).then_inc(s_ones, 1)
            pool.memset(neg_half[:, :], -0.5).then_inc(s_ones, 1)
            pool.memset(eps[:, :], EPS).then_inc(s_ones, 1)
            pool.dma_start(wk[:, :], WK).then_inc(ld_proj, 16)
            pool.dma_start(wq[:, :], WQ).then_inc(ld_proj, 16)
            pool.dma_start(wv[:, :], WV).then_inc(ld_proj, 16)
            for half in range(2):
                pool.dma_start(win[:, half, :], Win).then_inc(ld_in, 16)
                pool.dma_start(wout[half * M:(half + 1) * M, :], Wout).then_inc(ld_out, 16)
            pool.dma_start(bout_rep[:, :], bout.rearrange("(a n) -> a n", a=1).to_broadcast([P, P])).then_inc(ld_out, 16)
            pool.dma_start(wfc[:, :, :], W_fc.rearrange("(c p) d -> p c d", p=P)).then_inc(ld_ffn, 16)
            pool.dma_start(wpj[:, :, :], W_proj.rearrange("d (c h) -> d c h", c=HC)).then_inc(ld_ffn, 16)
            pool.memset(aTA[:, :, :], 0.0).then_inc(s_zero, 1)
            pool.memset(aTC[:, :, :], 0.0).then_inc(s_zero, 1)

            def rstd(ch, n, g):
                pool.wait_ge(ch["mv"], g + 1)
                pool.tensor_tensor(n["ve"][:, :], n["mv"][:, :, 1], eps[:, :], ALU.add).then_inc(ch["ve"], 1)
                pool.wait_ge(ch["ve"], g + 1)
                pool.tensor_tensor(n["rstd"][:, :], n["ve"][:, :], neg_half[:, :], ALU.pow).then_inc(ch["rstd"], 1)

            def normalise(ch, p, rs, a, g):
                pool.wait_ge(ch["rs"], g + 1)
                before(pool, ch["aT_mm"], g)
                pool.tensor_tensor(a[:, :, :].rearrange("p t (b j) -> p (t b) j", b=2),
                                   p[:, :, :].rearrange("p t (b j) -> p (t b) j", b=2),
                                   rs[:, :].unsqueeze(2).to_broadcast([P, 4, SK]), ALU.mult).then_inc(ch["a"], 1)

            def add_bout(g):
                before(pool, B["x"], g)
                pool.wait_ge(A["x"], g + 1)
                pool.tensor_tensor(tiles(xb[:, :]), tiles(xg(g)),
                                   bout_rep[:, :].unsqueeze(1).to_broadcast([P, GT, P]), ALU.add).then_inc(B["xb"], 1)

            pool.wait_ge(s_ones, 3)
            pool.wait_ge(ld_out, 48)

            def step(i):
                live = at_step(i)
                if live(0):
                    rstd(A, nA, i)
                if live(2):
                    add_bout(i - 2)
                if live(1):
                    rstd(B, nB, i - 1)
                if live(3):
                    normalise(C, pC, rsC, aC, i - 3)
                if live(0):
                    normalise(A, pA, rsA, aA, i)
                if live(2):
                    rstd(C, nC, i - 2)

            for i in range(K + 1):
                step(i)
            with pool.Fori(K + 1, NG) as i:
                step(i)
            for i in range(NG, NG + K):
                step(i)

            def add_out_bias(g):
                pool.wait_ge(C["x"], g + 1)
                if not isinstance(g, int) or g >= 1:
                    pool.wait_ge(E["x"], g)
                pool.tensor_tensor(tiles(xe[:, :]), tiles(xg(g)),
                                   out_bias[:, :].unsqueeze(1).to_broadcast([P, GT, P]), ALU.add).then_inc(E["xe"], 1)

            def rstd_hidden(g):
                pool.wait_ge(Dd["mv2"], GT * (g + 1))
                pool.tensor_tensor(veE[:, :], mvE[:, :, 1], eps[:, :], ALU.add).then_inc(E["ve"], 1)
                pool.wait_ge(E["ve"], g + 1)
                if not isinstance(g, int) or g >= 1:
                    pool.wait_ge(E["gn"], GT * g)
                pool.tensor_tensor(rsE[:, :], veE[:, :], neg_half[:, :], ALU.pow).then_inc(E["rstd"], 1)

            pool.wait_ge(s_ob_cp, 1)
            rstd(Dd, nD, 0)
            rstd(Dd, nD, 1)
            add_out_bias(0)
            rstd_hidden(0)
            with pool.Fori(1, NG - 1) as g:
                rstd(Dd, nD, g + 1)
                add_out_bias(g)
                rstd_hidden(g)
            add_out_bias(NG - 1)
            rstd_hidden(NG - 1)

        @block.scalar
        def _(act):
            act.wait_ge(s_rows0, 1)
            act.dma_start(rows[0:3, :], w_sim.rearrange("(a n) -> a n", a=3)).then_inc(ld_rows, 16)
            act.dma_start(rows[3:7, :], ln_w.rearrange("(a n) -> a n", a=HC)).then_inc(ld_rows, 16)
            act.dma_start(rows[7:11, :], ln_b.rearrange("(a n) -> a n", a=HC)).then_inc(ld_rows, 16)
            act.dma_start(rows[11:12, 0:M], b2.rearrange("(a n) -> a n", a=1)).then_inc(ld_rows, 16)
            for half in range(2):
                act.dma_start(rows[12:13, half * M:(half + 1) * M], bin_.rearrange("(a n) -> a n", a=1)).then_inc(ld_rows, 16)
                for src, dst in ((W1, w1_in), (b1, b1_in), (W2, w2_in)):
                    act.dma_start(dst[half * M:(half + 1) * M, :], src[:, half * HALF:(half + 1) * HALF]).then_inc(ld_inner, 16)
            act.wait_ge(s_rowsT, 1)
            act.activation(cols[:, :], bank[6][:, 0:13], ACT.Copy).then_inc(s_cols, 1)
            for half in range(2):
                act.wait_ge(s_cT_mm, half + 1)
                act.activation(cT[:, half * 512:(half + 1) * 512], bank[4 + half][:, :], ACT.Copy).then_inc(s_cT, 1)
            act.wait_ge(s_wk_mm, 1)
            act.activation(wkq[:, :], bank[7][:, 0:P], ACT.Copy, scale=SCALE).then_inc(s_wk, 1)
            act.activation(wvT[:, :], bank[7][:, P:2 * P], ACT.Copy).then_inc(s_wk, 1)
            act.wait_ge(ld_keys, 32)
            for half in range(2):
                act.wait_ge(s_keys_mm, 2 + half + 1)
                act.activation(rkey[:, half * 512:(half + 1) * 512], bank[half][:, :], ACT.Identity, bias=bsim[:, 0:1]).then_inc(s_rkey, 1)
            for n, dst in enumerate((projkey, values)):
                for half in range(2):
                    act.wait_ge(s_pv_mm, 2 * n + half + 1)
                    act.activation(dst[:, half * 512:(half + 1) * 512], bank[4 + 2 * n + half][:, :], ACT.Copy).then_inc(s_pv, 1)
            act.wait_ge(ld_inner, 96)
            act.wait_ge(s_b1s, 1)
            act.wait_ge(s_zero, 2)

            def evac_xT(ch, src, dst, g):
                act.wait_ge(ch["xT_mm"], g + 1)
                before(act, (B["s_mm"] if ch is B else ch["out_mm"]), g)
                act.activation(dst[:, :], src[:, :], ACT.Copy).then_inc(ch["xT"], 1)

            def exps(ch, sc, mx, p, sm, g):
                act.wait_ge(ch["mx"], g + 1)
                before(act, ch["a"], g)
                for t in range(2):
                    for b in range(2):
                        q = 2 * t + b
                        last = act.activation(p[:, t, b * SK:(b + 1) * SK], sc[:, t, b * SK:(b + 1) * SK], ACT.Exp,
                                              bias=mx[:, q:q + 1], accum_out=sm[:, q:q + 1])
                last.then_inc(ch["p"], 1)

            def evac_aT(ch, src, dst, g):
                act.wait_ge(ch["aT_mm"], g + 1)
                before(act, ch["out_mm"], g)
                for b in range(2):
                    rows_b = slice(b * SK, (b + 1) * SK)
                    last = act.activation(dst[rows_b, b, :], src[rows_b, 0:2 * P], ACT.Copy)
                last.then_inc(ch["aT"], 1)

            def batch_exps(g):
                act.wait_ge(A["msh"], g + 1)
                act.activation(eb[:, :], msh[:, :], ACT.Exp).then_inc(A["eb"], 1)

            def units(g, k):
                act.wait_ge(B["s_mm"], g + 1)
                if k < KP:
                    before(act, B["sum"], g, KP, k + 1 - KP)
                else:
                    before(act, B["acc"], g, KV, k - KP + 1 - KV)
                act.activation(u[:, k, :], bank[5][:, :], ACT.Relu, bias=b1_s[:, k:k + 1],
                               scale=w1_in[:, k:k + 1]).then_inc(B["uP"] if k < KP else B["uV"], 1)

            def transposed_weights():
                act.wait_ge(s_fcT, 1)
                act.activation(wfcT[:, :], bank[6][:, :], ACT.Copy).then_inc(s_fcT_cp, 1)
                act.wait_ge(s_pjT, 1)
                act.activation(wpjT[:, :, :].rearrange("p c d -> p (c d)"), bank[5][:, :], ACT.Copy).then_inc(s_pjT_cp, 1)
                act.wait_ge(s_ob, 1)
                act.activation(out_bias[:, :], bank[6][:, 0:P], ACT.Copy).then_inc(s_ob_cp, 1)

            def step(i):
                live = at_step(i)
                if live(2):
                    units(i - 2, KP + 0)
                    units(i - 2, 0)
                    units(i - 2, KP + 1)
                    units(i - 2, 1)
                if live(3):
                    evac_xT(C, bank[1], xTC, i - 3)
                if live(0):
                    evac_xT(A, bank[0], xTA, i)
                if live(2):
                    units(i - 2, KP + 2)
                    units(i - 2, 2)
                    units(i - 2, KP + 3)
                    units(i - 2, 3)
                if live(3):
                    exps(C, scoresC, mxC, pC, smC, i - 3)
                if live(0):
                    exps(A, simA, mxA, pA, smA, i)
                    batch_exps(i)
                if live(3):
                    evac_aT(C, bank[3], aTC, i - 3)
                if live(0):
                    evac_aT(A, bank[2], aTA, i)
                if live(1):
                    evac_xT(B, bank[5], xTB, i - 1)

            for i in range(K + 1):
                step(i)
                if i == 0:
                    transposed_weights()
            with act.Fori(K + 1, NG) as i:
                step(i)
            for i in range(NG, NG + K):
                step(i)

            def high_half(g):
                act.wait_ge(Dd["xT_mm"], g + 1)
                if not isinstance(g, int) or g >= 1:
                    act.wait_ge(Dd["fc_mm"], GT * g)
                act.activation(hiD[:, :], bank[0][:, :], ACT.Copy).then_inc(Dd["xT"], 1)

            def gelu(g, k):
                act.wait_ge(Dd["fc_mm"], GT * g + k + 1)
                if not isinstance(g, int) or g >= 1:
                    act.wait_ge(E["gn"], GT * (g - 1) + k + 1)
                act.activation(gel[:, k, :], bank[1 + k % 2][:, :], ACT.Gelu).then_inc(Dd["gel"], 1)

            def evac_gT(g, k):
                act.wait_ge(E["gT_mm"], GT * g + k + 1)
                act.activation(gnT[:, k, :], bank[3 + k % 2][:, :], ACT.Copy).then_inc(E["gT"], 1)

            def step2(i, d, e):
                if d:
                    high_half(i)
                for k in range(GT):
                    if e:
                        evac_gT(i - 1, k)
                    if d:
                        gelu(i, k)

            step2(0, True, False)
            with act.Fori(1, NG) as i:
                step2(i, True, True)
            step2(NG, False, True)

        @block.vector
        def _(dve):
            def stats(ch, n, g):
                if ch is A:
                    wait_alone("dve", dve, ld_x, 16 * (g + 1))
                else:
                    wait_alone("dve", dve, (A if ch is B else B)["x"], g + 1)
                for k in range(GT):
                    dve.bn_stats(n["stats"][:, k, :], xtile(g, k)).then_inc(ch["bn"], 1)

            def aggregate(ch, n, g):
                wait_alone("dve", dve, ch["bn"], GT * (g + 1))
                for k in range(GT):
                    last = dve.bn_aggr(n["mv"][:, k, :], n["stats"][:, k, :])
                last.then_inc(ch["mv"], 1)

            def norm(ch, n, g):
                dve.wait_ge(ch["rstd"], g + 1)
                before(dve, A["hc_mm"] if ch is A else ch["xT_mm"], g)
                for k in range(GT):
                    last = dve.tensor_scalar(n["xn"][:, k * P:(k + 1) * P], xtile(g, k), n["mv"][:, k, 0:1],
                                             n["rstd"][:, k:k + 1], ALU.subtract, ALU.mult)
                last.then_inc(ch["xn"], 1)

            def key_term(g):
                dve.wait_ge(A["s_mm"], g + 1)
                before(dve, A["p"], g)
                dve.tensor_tensor(simA[:, :, :], bank[2][:, 0:2 * P].rearrange("p (t n) -> p t n", t=2),
                                  keys_of(rkey, g).unsqueeze(1).to_broadcast([P, 2, P]), ALU.add).then_inc(A["sim"], 1)

            def row_max(ch, sc, mx, g):
                dve.wait_ge(ch["sim"] if ch is A else ch["s_mm"], g + 1)
                before(dve, ch["mxT_mm"] if ch is A else ch["p"], g)
                dve.tensor_reduce(mx[:, :], sc[:, :, :].rearrange("p t (b j) -> p (t b) j", b=2), AX_X, ALU.max,
                                  negate=True).then_inc(ch["mx"], 1)

            def row_scale(ch, sm, rs, g):
                dve.wait_ge(ch["p"], g + 1)
                dve.reciprocal(rs[:, :], sm[:, :]).then_inc(ch["rs"], 1)

            def tile_max(g):
                dve.wait_ge(A["mxT_mm"], g + 1)
                dve.tensor_reduce(m4[:, :], bank[4][0:4, 0:P], AX_X, ALU.min).then_inc(A["m4"], 1)

            def tile_max_diagonal(g):
                dve.wait_ge(A["m4"], g + 1)
                dve.tensor_scalar(m4d[:, :], ident[0:4, 0:4], m4[:, 0:1], None, ALU.mult).then_inc(A["m4d"], 1)

            def batch_max(g):
                dve.wait_ge(A["gm_mm"], g + 1)
                dve.tensor_reduce(gmax[:, :], bank[4][:, P:P + 4].rearrange("p (t b) -> p b t", b=2), AX_X,
                                  ALU.min).then_inc(A["gmax"], 1)

            def batch_shift(g):
                dve.wait_ge(A["gmax"], g + 1)
                dve.tensor_tensor(msh[:, :].rearrange("p (t b) -> p t b", b=2),
                                  gmax[:, :].unsqueeze(1).to_broadcast([P, 2, 2]),
                                  mxA[:, :].rearrange("p (t b) -> p t b", b=2), ALU.subtract).then_inc(A["msh"], 1)

            def batch_scale(g):
                dve.wait_ge(A["hc_mm"], g + 1)
                dve.reciprocal(erec[:, :], bank[4][:, P + 4:P + 6]).then_inc(A["erec"], 1)

            def batch_mean(g):
                dve.wait_ge(A["erec"], g + 1)
                dve.tensor_tensor(hc[:, :], bank[4][:, P + 8:P + 10], erec[:, :], ALU.mult).then_inc(A["hc"], 1)

            def fold_mean(g):
                dve.wait_ge(A["hc"], g + 1)
                before(dve, A["out_mm"], g)
                for b in range(2):
                    last = dve.scalar_tensor_tensor(w14[:, b, :], wqv[:, 3, :], hc[:, b:b + 1], wqv[:, 0, :],
                                                    ALU.mult, ALU.add)
                last.then_inc(A["w14"], 1)

            def product(g):
                dve.wait_ge(A["hq_mm"], g + 1)
                before(dve, A["out_mm"], g)
                dve.tensor_tensor(prodT[:, :], bank[4][:, :], xTA[:, :], ALU.mult).then_inc(A["prod"], 1)

            def sum_pair(g, k):
                dve.wait_ge(B["uV"], KV * g + k + 1)
                w = w2_in[:, KP + k:KP + k + 1]
                if k == 0:
                    before(dve, B["out_mm"], g)
                    dve.tensor_scalar(acc[:, :], u[:, KP, :], w, b2_half[:, 0:1], ALU.mult, ALU.add).then_inc(B["acc"], 1)
                else:
                    dve.wait_ge(B["acc"], KV * g + k)
                    dve.scalar_tensor_tensor(acc[:, :], u[:, KP + k, :], w, acc[:, :], ALU.mult, ALU.add).then_inc(B["acc"], 1)

            def residual(ch, g):
                dve.wait_ge(ch["out_mm"], g + 1)
                dve.tensor_tensor(xg(g), bank[7 if ch is A else 1][:, :], xg(g), ALU.add).then_inc(ch["x"], 1)

            def residual_ffn(g):
                dve.wait_ge(B["out_mm"], g + 1)
                dve.wait_ge(B["xb"], g + 1)
                dve.tensor_tensor(xg(g), bank[6][:, :], xb[:, :], ALU.add).then_inc(B["x"], 1)

            dve.wait_ge(s_cols, 1)
            dve.wait_ge(s_ones, 1)
            dve.tensor_scalar(w2_rep[:, :], ones[:, :], w2_sim, None, ALU.mult).then_inc(s_w2rep, 1)
            dve.wait_ge(s_cT, 2)
            dve.tensor_scalar(simkey[:, :], cT[:, :], w3_sim, w1_sim, ALU.mult, ALU.add).then_inc(s_simkey, 1)
            dve.wait_ge(ld_keys, 32)
            for half in range(2):
                dve.wait_ge(s_keys_mm, half + 1)
                dve.tensor_tensor(tiles(cw2[:, half * 512:(half + 1) * 512]), tiles(bank[2 + half][:, :]),
                                  bqv_rep[:, :].unsqueeze(1).to_broadcast([P, 4, P]), ALU.add).then_inc(s_cw2, 1)
            dve.wait_ge(ld_inner, 96)
            dve.scalar_tensor_tensor(b1_s[:, :], w1_in[:, :], bin_col, b1_in[:, :], ALU.mult, ALU.add).then_inc(s_b1s, 1)
            dve.tensor_scalar(b2_half[:, :], b2_col, 1.0, None, ALU.mult).then_inc(s_b1, 1)
            dve.wait_ge(ld_qv, 16)
            dve.wait_ge(s_ident, 1)
            dve.wait_ge(s_b1, 1)
            dve.wait_ge(s_rkey, 2)

            def step(i):
                live = at_step(i)
                if live(0):
                    stats(A, nA, i)
                if live(1):
                    product(i - 1)
                if live(0):
                    aggregate(A, nA, i)
                if live(3):
                    norm(C, nC, i - 3)
                if live(2):
                    sum_pair(i - 2, 0)
                if live(0):
                    norm(A, nA, i)
                if live(2):
                    sum_pair(i - 2, 1)
                if live(1):
                    residual(A, i - 1)
                    stats(B, nB, i - 1)
                    aggregate(B, nB, i - 1)
                if live(0):
                    key_term(i)
                    row_max(A, simA, mxA, i)
                if live(3):
                    row_max(C, scoresC, mxC, i - 3)
                if live(2):
                    sum_pair(i - 2, 2)
                if live(0):
                    tile_max(i)
                    tile_max_diagonal(i)
                if live(2):
                    sum_pair(i - 2, 3)
                if live(0):
                    batch_max(i)
                if live(3):
                    row_scale(C, smC, rsC, i - 3)
                if live(0):
                    batch_shift(i)
                if live(1):
                    norm(B, nB, i - 1)
                if live(0):
                    row_scale(A, smA, rsA, i)
                if live(2):
                    residual_ffn(i - 2)
                    stats(C, nC, i - 2)
                if live(0):
                    batch_scale(i)
                    batch_mean(i)
                if live(2):
                    aggregate(C, nC, i - 2)
                if live(0):
                    fold_mean(i)
                if live(3):
                    residual(C, i - 3)

            def folded_output():
                dve.wait_ge(ld_out, 48)
                for k in range(KP):
                    dve.tensor_scalar(wsum[:, k, :], wout[:, :], w2_in[:, k:k + 1], None, ALU.mult).then_inc(s_wsum, 1)

            def quantise():
                dve.wait_ge(ld_ffn, 32)
                for k, w in enumerate((wfc, wpj)):
                    dve.tensor_reduce(absum[:, k:k + 1], w[:, :, :].rearrange("p c d -> p (c d)"), AX_X, ALU.add,
                                      apply_absolute_value=True).then_inc(s_absum, 1)
                dve.wait_ge(s_absum_mm, 1)
                dve.tensor_scalar(gamma[:, :], bank[6][:, 16:18], 1.0 / (HID * D), ABSMEAN_EPS, ALU.mult, ALU.add).then_inc(s_gamma, 1)
                dve.wait_ge(s_gamma, 1)
                dve.reciprocal(inv_gamma[:, :], gamma[:, :]).then_inc(s_igamma, 1)
                dve.wait_ge(s_igamma, 1)
                for k, w in enumerate((wfc, wpj)):
                    flat = w[:, :, :].rearrange("p c d -> p (c d)")
                    dve.tensor_scalar(above[:, k, :], flat, inv_gamma[:, k:k + 1], 0.5, ALU.mult, ALU.is_gt).then_inc(s_above, 1)
                    dve.tensor_scalar(below[:, k, :], flat, inv_gamma[:, k:k + 1], -0.5, ALU.mult, ALU.is_lt).then_inc(s_above, 1)
                    dve.wait_ge(s_above, 2 * (k + 1))
                    dve.tensor_tensor(flat, above[:, k, :], below[:, k, :], ALU.subtract).then_inc(s_quant, 1)
                for c in range(HC):
                    dve.tensor_scalar(lnb_rep[:, c, :], ones[:, :], lnb_col[c], None, ALU.mult).then_inc(s_lnb, 1)
                dve.wait_ge(s_pjT_cp, 1)
                for c in range(HC):
                    dve.tensor_scalar(wpjT_ln[:, c, :], wpjT[:, c, :], lnw_col[c], None, ALU.mult).then_inc(s_pjln, 1)

            for i in range(K + 1):
                step(i)
                if i == 0:
                    folded_output()
                    quantise()
            with dve.Fori(K + 1, NG) as i:
                step(i)
            for i in range(NG, NG + K):
                step(i)

            def low_half(g):
                dve.wait_ge(Dd["xT"], g + 1)
                dve.tensor_tensor(loD[:, :], bank[0][:, :], hiD[:, :], ALU.subtract).then_inc(Dd["lo"], 1)

            def hidden_stats(g, k):
                wait_alone("dve", dve, Dd["gel"], GT * g + k + 1)
                dve.bn_stats(statsE[:, k, :], gel[:, k, :]).then_inc(Dd["bn2"], 1)

            def hidden_aggr(g):
                wait_alone("dve", dve, Dd["bn2"], GT * (g + 1))
                for k in range(GT):
                    dve.bn_aggr(mvE[:, k, :], statsE[:, k, :]).then_inc(Dd["mv2"], 1)

            def hidden_norm(g, k):
                dve.tensor_scalar(gn[:, k, :], gel[:, k, :], mvE[:, k, 0:1], rsE[:, k:k + 1],
                                  ALU.subtract, ALU.mult).then_inc(E["gn"], 1)

            def step2(i, d, e):
                if e:
                    dve.wait_ge(E["rstd"], i)
                    for k in range(GT):
                        hidden_norm(i - 1, k)
                if d:
                    low_half(i)
                    for k in range(GT):
                        hidden_stats(i, k)
                    hidden_aggr(i)
                if e:
                    dve.wait_ge(E["out_mm"], i)
                    dve.wait_ge(E["xe"], i)
                    dve.tensor_tensor(xg(i - 1), bank[5][:, :], xe[:, :], ALU.add).then_inc(E["x"], 1)

            def stats_norm(g):
                wait_alone("dve", dve, C["x"], g + 1)
                for k in range(GT):
                    dve.bn_stats(nD["stats"][:, k, :], xtile(g, k)).then_inc(Dd["bn"], 1)
                aggregate(Dd, nD, g)
                norm(Dd, nD, g)

            stats_norm(0)
            step2(0, True, False)
            stats_norm(1)
            with dve.Fori(1, NG - 1) as i:
                step2(i, True, True)
                stats_norm(i + 1)
            step2(NG - 1, True, True)
            step2(NG, False, True)

        @block.tensor
        def _(pe):
            def xT(ch, n, dst, g):
                pe.wait_ge(ch["xn"], g + 1)
                if ch is A:
                    before(pe, A["xT"], g)
                elif ch is B:
                    before(pe, B["uP"], g, KP)
                    before(pe, B["uV"], g, KV)
                elif ch is C:
                    before(pe, C["x"], g)
                for k in range(GT):
                    last = pe.transpose(dst[:, k * P:(k + 1) * P], n["xn"][:, k * P:(k + 1) * P], ident[:, :])
                last.then_inc(ch["xT_mm"], 1)

            def scores(ch, xt, keys, dst, g):
                pe.wait_ge(ch["xT"], g + 1)
                before(pe, ch["aT"], g)
                for t in range(2):
                    for b in range(2):
                        k = 2 * b + t
                        last = pe.matmul(dst[:, t * P + b * SK:t * P + (b + 1) * SK], xt[:, k * P:(k + 1) * P],
                                         keys[:, bass.ds(g * P + b * SK, SK)], start=True, stop=True)
                last.then_inc(ch["s_mm"], 1)

            def aT(ch, a, dst, g):
                pe.wait_ge(ch["a"], g + 1)
                for t in range(2):
                    last = pe.transpose(dst[:, t * P:(t + 1) * P], a[:, t, :], ident[:, :])
                last.then_inc(ch["aT_mm"], 1)

            def turn_max(g):
                pe.wait_ge(A["mx"], g + 1)
                before(pe, A["prod"], g)
                pe.transpose(bank[4][0:4, 0:P], mxA[:, :], ident[:, :]).then_inc(A["mxT_mm"], 1)

            def spread_max(g):
                pe.wait_ge(A["m4d"], g + 1)
                pe.matmul(bank[4][:, P:P + 4], ones[0:4, :], m4d[:, :], start=True, stop=True).then_inc(A["gm_mm"], 1)

            def batch_sums(g):
                pe.wait_ge(A["eb"], g + 1)
                for t in range(2):
                    pe.matmul(bank[4][:, P + 4:P + 6], ones[:, :], eb[:, 2 * t:2 * t + 2], start=(t == 0), stop=(t == 1))
                for b in range(2):
                    for t in range(2):
                        k = 2 * b + t
                        last = pe.matmul(bank[4][:, P + 8 + b:P + 9 + b], nA["xn"][:, k * P:(k + 1) * P],
                                         eb[:, 2 * t + b:2 * t + b + 1], start=(t == 0), stop=(t == 1))
                last.then_inc(A["hc_mm"], 1)

            def attended(g):
                pe.wait_ge(A["aT"], g + 1)
                pe.wait_ge(A["hc"], g + 1)
                pe.wait_ge(A["ctx"], 16 * (g + 1))
                for b in range(2):
                    last = pe.matmul(bank[4][:, b * 2 * P:(b + 1) * 2 * P], ctxA[:, :], aTA[:, b, :], start=True, stop=True)
                last.then_inc(A["hq_mm"], 1)

            def outA(g, k):
                b, t = k // 2, k % 2
                if k == 0:
                    pe.wait_ge(A["prod"], g + 1)
                    pe.wait_ge(A["w14"], g + 1)
                    before(pe, A["x"], g)
                o = bank[7][:, k * P:(k + 1) * P]
                pe.matmul(o, aTA[:, b, t * P:(t + 1) * P], keys_of(cw2, g), start=True, stop=False)
                pe.matmul(o, xTA[:, k * P:(k + 1) * P], w14[:, b, :], start=False, stop=False)
                last = pe.matmul(o, prodT[:, k * P:(k + 1) * P], wqv[:, 2, :], start=False, stop=True)
                if k == GT - 1:
                    last.then_inc(A["out_mm"], 1)

            def inner(g):
                pe.wait_ge(B["xT"], g + 1)
                pe.matmul(bank[5][:, :], win[:, :, :].rearrange("p a m -> p (a m)"), xTB[:, :], start=True, stop=True)\
                    .then_inc(B["s_mm"], 1)

            def sum_units(g, k):
                pe.wait_ge(B["uP"], KP * g + k + 1)
                if k == 0:
                    before(pe, B["x"], g)
                for j in range(GT):
                    last = pe.matmul(bank[6][:, j * P:(j + 1) * P], u[:, k, j * P:(j + 1) * P], wsum[:, k, :],
                                     start=(k == 0 and j == 0), stop=False, skip_group_check=True)
                last.then_inc(B["sum"], 1)

            def outB(g):
                pe.wait_ge(B["acc"], KV * (g + 1))
                for j in range(GT):
                    last = pe.matmul(bank[6][:, j * P:(j + 1) * P], acc[:, j * P:(j + 1) * P], wout[:, :],
                                     start=False, stop=True, skip_group_check=True)
                last.then_inc(B["out_mm"], 1)

            def outC(g):
                pe.wait_ge(C["aT"], g + 1)
                for k in range(GT):
                    b, t = k // 2, k % 2
                    last = pe.matmul(bank[1][:, k * P:(k + 1) * P], aTC[:, b, t * P:(t + 1) * P], keys_of(values, g),
                                     start=True, stop=True)
                last.then_inc(C["out_mm"], 1)

            pe.wait_ge(s_ident, 1)
            pe.wait_ge(ld_ctx, 16)
            for g in range(NG):
                last = pe.transpose(bank[4 + g // 4][:, g % 4 * P:(g % 4 + 1) * P], CTX[:, g * P:(g + 1) * P], ident[:, :])
                if g % 4 == 3:
                    last.then_inc(s_cT_mm, 1)
            pe.wait_ge(ld_rows, 96)
            pe.transpose(bank[6][:, 0:13], rows[:, :], ident[0:13, 0:13]).then_inc(s_rowsT, 1)
            pe.wait_ge(ld_qv, 16)
            pe.wait_ge(s_cT, 2)
            for g in range(NG):
                last = pe.matmul(bank[2 + g // 4][:, g % 4 * P:(g % 4 + 1) * P], cT[:, g * P:(g + 1) * P], wqv[:, 1, :],
                                 start=True, stop=True)
                if g % 4 == 3:
                    last.then_inc(s_keys_mm, 1)
            pe.wait_ge(s_w2rep, 1)
            for half in range(2):
                pe.matmul(bank[half][:, :], w2_rep[:, :], cT[:, half * 512:(half + 1) * 512], start=True, stop=True)\
                    .then_inc(s_keys_mm, 1)
            pe.wait_ge(ld_proj, 48)
            pe.matmul(bank[7][:, 0:P], wk[:, :], wq[:, :], start=True, stop=True)
            pe.transpose(bank[7][:, P:2 * P], wv[:, :], ident[:, :]).then_inc(s_wk_mm, 1)
            pe.wait_ge(s_wk, 2)
            for half in range(2):
                pe.matmul(bank[4 + half][:, :], wkq[:, :], cT[:, half * 512:(half + 1) * 512], start=True, stop=True)\
                    .then_inc(s_pv_mm, 1)
            for g in range(NG):
                last = pe.matmul(bank[6 + g // 4][:, g % 4 * P:(g % 4 + 1) * P], cT[:, g * P:(g + 1) * P], wvT[:, :],
                                 start=True, stop=True)
                if g % 4 == 3:
                    last.then_inc(s_pv_mm, 1)
            pe.wait_ge(s_rkey, 2)
            pe.wait_ge(s_cw2, 2)
            pe.wait_ge(s_simkey, 1)
            pe.wait_ge(s_pv, 4)
            pe.wait_ge(s_wk, 2)
            pe.wait_ge(ld_in, 32)
            pe.wait_ge(ld_out, 48)
            pe.wait_ge(s_ones, 1)

            def step(i):
                live = at_step(i)
                if live(1):
                    attended(i - 1)
                if live(2):
                    inner(i - 2)
                if live(1):
                    outA(i - 1, 0)
                    outA(i - 1, 1)
                    outA(i - 1, 2)
                if live(3):
                    xT(C, nC, bank[1], i - 3)
                if live(1):
                    outA(i - 1, 3)
                if live(0):
                    xT(A, nA, bank[0], i)
                if live(2):
                    sum_units(i - 2, 0)
                if live(0):
                    scores(A, xTA, simkey, bank[2], i)
                if live(3):
                    scores(C, xTC, projkey, bank[3], i - 3)
                if live(2):
                    sum_units(i - 2, 1)
                if live(0):
                    turn_max(i)
                if live(2):
                    sum_units(i - 2, 2)
                if live(0):
                    spread_max(i)
                if live(2):
                    sum_units(i - 2, 3)
                    outB(i - 2)
                if live(3):
                    aT(C, aC, bank[3], i - 3)
                if live(0):
                    batch_sums(i)
                    aT(A, aA, bank[2], i)
                if live(3):
                    outC(i - 3)
                if live(1):
                    xT(B, nB, bank[5], i - 1)

            def quantised():
                pe.wait_ge(s_absum, 2)
                pe.matmul(bank[6][:, 16:18], ones[:, :], absum[:, :], start=True, stop=True).then_inc(s_absum_mm, 1)
                pe.wait_ge(s_quant, 1)
                for c in range(HC):
                    last = pe.transpose(bank[6][:, c * P:(c + 1) * P], wfc[:, c, :], ident[:, :])
                last.then_inc(s_fcT, 1)
                pe.wait_ge(s_quant, 2)
                for c in range(HC):
                    last = pe.transpose(bank[5][:, c * P:(c + 1) * P], wpj[:, c, :], ident[:, :])
                last.then_inc(s_pjT, 1)
                pe.wait_ge(s_pjT_cp, 1)
                pe.wait_ge(s_fcT_cp, 1)
                pe.wait_ge(s_lnb, HC)
                for c in range(HC):
                    last = pe.matmul(bank[6][:, 0:P], lnb_rep[:, c, :], wpjT[:, c, :], start=(c == 0), stop=(c == HC - 1))
                last.then_inc(s_ob, 1)
                pe.wait_ge(s_ob_cp, 1)

            for i in range(K + 1):
                step(i)
                if i == 0:
                    quantised()
                    pe.wait_ge(s_wsum, KP)
            with pe.Fori(K + 1, NG) as i:
                step(i)
            for i in range(NG, NG + K):
                step(i)

            def up(g, k):
                n = GT * g + k
                if k >= 2 or not isinstance(g, int) or g >= 1:
                    pe.wait_ge(Dd["gel"], n - 1)
                o = bank[1 + k % 2][:, :]
                pe.matmul(o, hiD[:, k * P:(k + 1) * P], wfcT[:, :], start=True, stop=False)
                pe.matmul(o, loD[:, k * P:(k + 1) * P], wfcT[:, :], start=False, stop=True).then_inc(Dd["fc_mm"], 1)

            def turn(g, k):
                n = GT * g + k
                pe.wait_ge(E["gn"], n + 1)
                if k >= 2 or not isinstance(g, int) or g >= 1:
                    pe.wait_ge(E["gT"], n - 1)
                for c in range(HC):
                    last = pe.transpose(bank[3 + k % 2][:, c * P:(c + 1) * P], gn[:, k, c * P:(c + 1) * P], ident[:, :])
                last.then_inc(E["gT_mm"], 1)

            def down(g, k):
                pe.wait_ge(E["gT"], GT * g + k + 1)
                if k == 0 and (not isinstance(g, int) or g >= 1):
                    pe.wait_ge(E["x"], g)
                for c in range(HC):
                    last = pe.matmul(bank[5][:, k * P:(k + 1) * P], gnT[:, k, c * P:(c + 1) * P], wpjT_ln[:, c, :],
                                     start=(c == 0), stop=(c == HC - 1))
                if k == GT - 1:
                    last.then_inc(E["out_mm"], 1)

            def step2(i, d, e):
                if d:
                    if not isinstance(i, int) or i >= 1:
                        pe.wait_ge(Dd["lo"], i)
                    xT(Dd, nD, bank[0], i)
                for k in range(GT):
                    if e:
                        turn(i - 1, k)
                    if d:
                        if k == 0:
                            pe.wait_ge(Dd["lo"], i + 1)
                        up(i, k)
                    if e and k >= 1:
                        down(i - 1, k - 1)
                if e:
                    down(i - 1, GT - 1)

            pe.wait_ge(s_pjln, HC)
            step2(0, True, False)
            step2(1, True, True)
            with pe.Fori(2, NG) as i:
                step2(i, True, True)
            step2(NG, False, True)


_INS = ["x", "ctx_1024", "L0_xattn_w_sim", "L0_xattn_b_sim", "L0_xattn_W_qv", "L0_xattn_b_qv", "L0_ffn_Win",
        "L0_ffn_bin_", "L0_ffn_W1", "L0_ffn_b1", "L0_ffn_W2", "L0_ffn_b2", "L0_ffn_Wout", "L0_ffn_bout",
        "L1_xattn_WQ", "L1_xattn_WK", "L1_xattn_WV", "L1_ffn_W_fc", "L1_ffn_ln_w", "L1_ffn_ln_b",
        "L1_ffn_W_proj"]


def kernel(**inputs):
    import numpy as np
    import concourse.bacc as bacc
    from concourse.bass_utils import run_bass_kernel_spmd

    nc = bacc.Bacc("TRN2", target_bir_lowering=False, num_devices=1)
    arrays, args = {}, []
    for name in _INS:
        a = np.ascontiguousarray(inputs[name])
        arrays[f"in_{name}"] = a
        args.append(nc.dram_tensor(f"in_{name}", a.shape, mybir.dt.from_np(a.dtype), kind="ExternalInput").ap())
    shape = inputs["x"].shape
    out = nc.dram_tensor("out_0", shape, F32, kind="ExternalOutput").ap()
    xattn_ffn_stack(nc, *args, out)
    r = run_bass_kernel_spmd(nc, [arrays], core_ids=[0])
    return r.results[0]["out_0"]
```

```python
from contextlib import ExitStack

import concourse.bass as bass
from concourse import mybir

P = 128
GT = 4
EPS = 1e-5
ABSMEAN_EPS = 1e-6

ALU = mybir.AluOpType
ACT = mybir.ActivationFunctionType
F32 = mybir.dt.float32
F16 = mybir.dt.float16
AX_X = mybir.AxisListType.X


def xattn_ffn_stack(nc, x, ctx, w_sim, b_sim, W_qv, b_qv, Win, bin_, W1, b1, W2, b2, Wout, bout,
                    WQ, WK, WV, W_fc, ln_w, ln_b, W_proj, out):
    NB, S, D = x.shape
    SK = ctx.shape[1]
    NG = NB // 2
    M, INNER = W1.shape
    HID = W_fc.shape[0]
    HC = HID // P
    assert D == P and S == 2 * P and SK == 64 and M == 64 and HC == 4
    GC = GT * P
    SCALE = float(D) ** -0.5
    HALF = INNER // 2
    KP = 4
    KV = HALF - KP
    K = 3
    K2 = 3
    DVE_TILES, ACT_TILES = (0, 2), (1, 3)
    NV, NA = len(DVE_TILES), len(ACT_TILES)

    with ExitStack() as es:
        def sb(name, shape, dt=F32):
            return es.enter_context(nc.sbuf_tensor(name, shape, dt))

        def sem(name):
            return es.enter_context(nc.semaphore(name))

        bank = [es.enter_context(nc.psum_tensor(f"bank{i}", [P, 512], F32)) for i in range(8)]

        X = sb("X", [P, NG * GC])
        CTX = sb("CTX", [P, NG * P])

        ident = sb("ident", [P, P])
        ones = sb("ones", [P, P])
        neg_half = sb("neg_half", [P, GT])
        eps = sb("eps", [P, GT])
        rows = sb("rows", [13, P])
        cols = sb("cols", [P, 13])
        w1_sim, w2_sim, w3_sim = cols[:, 0:1], cols[:, 1:2], cols[:, 2:3]
        lnw_col = [cols[:, 3 + c:4 + c] for c in range(HC)]
        lnb_col = [cols[:, 7 + c:8 + c] for c in range(HC)]
        b2_col, bin_col = cols[:, 11:12], cols[:, 12:13]
        w1_in = sb("w1_in", [P, HALF])
        b1_in = sb("b1_in", [P, HALF])
        w2_in = sb("w2_in", [P, HALF])
        b1_s = sb("b1_s", [P, HALF])
        b2_half = sb("b2_half", [P, 1])
        wqv = sb("wqv", [P, 4, P])
        bqv_rep = sb("bqv_rep", [P, P])
        bsim = sb("bsim", [P, 1])
        win = sb("win", [P, 2, M])
        wout = sb("wout", [P, P])
        bout_rep = sb("bout_rep", [P, P])
        wq, wk, wv = sb("wq", [P, P]), sb("wk", [P, P]), sb("wv", [P, P])
        wfc = sb("wfc", [P, HC, P])
        wpj = sb("wpj", [P, HC, P])
        w2_rep = sb("w2_rep", [P, P])
        wkq = sb("wkq", [P, P])
        wvT = sb("wvT", [P, P])
        wsum = sb("wsum", [P, KP, P])
        cT = sb("cT", [P, NG * P])
        simkey = sb("simkey", [P, NG * P])
        rkey = sb("rkey", [P, NG * P])
        cw2 = sb("cw2", [P, NG * P])
        projkey = sb("projkey", [P, NG * P])
        values = sb("values", [P, NG * P])
        absum = sb("absum", [P, 2])
        gamma = sb("gamma", [P, 2])
        inv_gamma = sb("inv_gamma", [P, 2])
        above = sb("above", [P, 2, HID])
        below = sb("below", [P, 2, HID])
        wfcT = sb("wfcT", [P, HID], F16)
        wpjT = sb("wpjT", [P, HC, P])
        wpjT_ln = sb("wpjT_ln", [P, HC, P])
        lnb_rep = sb("lnb_rep", [P, HC, P])
        out_bias = sb("out_bias", [P, P])

        def norm_set(c):
            return {"stats": sb(f"stats{c}", [P, GT, 6]), "mv": sb(f"mv{c}", [P, GT, 2]),
                    "ve": sb(f"ve{c}", [P, GT]), "rstd": sb(f"rstd{c}", [P, GT]),
                    "xn": sb(f"xn{c}", [P, GC])}

        nA, nB, nC, nD = norm_set("A"), norm_set("B"), norm_set("C"), norm_set("D")
        shiftB = sb("shiftB", [P, GT])
        xTA, xTB, xTC = sb("xTA", [P, GC]), sb("xTB", [P, GC]), sb("xTC", [P, GC])
        ctxA = sb("ctxA", [P, P])
        simA = sb("simA", [P, 2, P])
        mxA, mxC = sb("mxA", [P, 4]), sb("mxC", [P, 4])
        pA, pC = sb("pA", [P, 2, P]), sb("pC", [P, 2, P])
        smA, smC = sb("smA", [P, 4]), sb("smC", [P, 4])
        rsA, rsC = sb("rsA", [P, 4]), sb("rsC", [P, 4])
        aA, aC = sb("aA", [P, 2, P]), sb("aC", [P, 2, P])
        aTA, aTC = sb("aTA", [P, 2, 2 * P]), sb("aTC", [P, 2, 2 * P])
        m4 = sb("m4", [4, 1])
        m4d = sb("m4d", [4, 4])
        gmax = sb("gmax", [P, 2])
        msh = sb("msh", [P, 4])
        eb = sb("eb", [P, 4])
        erec = sb("erec", [P, 2])
        hc = sb("hc", [P, 2])
        w14 = sb("w14", [P, 2, P])
        prodT = sb("prodT", [P, GC])
        u = sb("u", [P, HALF, GC])
        acc = sb("acc", [P, GC])
        xb = sb("xb", [P, GC])
        hiD = sb("hiD", [P, GC], F16)
        loD = sb("loD", [P, GC], F16)
        gel = sb("gel", [P, GT, HID])
        statsE = sb("statsE", [P, GT, 6])
        mvE = sb("mvE", [P, GT, 2])
        veE = sb("veE", [P, GT])
        rsE = sb("rsE", [P, GT])
        shiftE = sb("shiftE", [P, GT])
        gn = sb("gn", [P, GT, HID])
        gnT = sb("gnT", [P, GT, HID])
        xe = sb("xe", [P, GC])

        scoresC = bank[3][:, 0:2 * P].rearrange("p (t n) -> p t n", t=2)

        ld_x = sem("ld_x")
        ld_ctx, ld_rows, ld_inner, ld_qv, ld_keys, ld_in, ld_out, ld_proj, ld_ffn = (
            sem(n) for n in ("ld_ctx", "ld_rows", "ld_inner", "ld_qv", "ld_keys", "ld_in", "ld_out",
                             "ld_proj", "ld_ffn"))
        stored = sem("stored")
        (s_zero, s_ones, s_id0, s_ident, s_rows0, s_rowsT, s_cols, s_w2rep, s_b1, s_b1s, s_wsum, s_wk_mm, s_wk,
         s_cT_mm, s_cT, s_simkey, s_cw2_mm, s_rkey_mm, s_rkey, s_cw2, s_proj_mm, s_proj, s_val_mm, s_val,
         s_absum, s_absum_mm, s_gamma, s_igamma, s_above, s_quant, s_fcT, s_fcT_cp, s_pjT, s_pjT_cp,
         s_lnb, s_ob, s_ob_cp, s_pjln) = (
            sem(n) for n in ("s_zero", "s_ones", "s_id0", "s_ident", "s_rows0", "s_rowsT", "s_cols", "s_w2rep",
                             "s_b1", "s_b1s", "s_wsum", "s_wk_mm", "s_wk", "s_cT_mm", "s_cT", "s_simkey",
                             "s_cw2_mm", "s_rkey_mm", "s_rkey", "s_cw2", "s_proj_mm", "s_proj", "s_val_mm", "s_val",
                             "s_absum", "s_absum_mm", "s_gamma", "s_igamma", "s_above", "s_quant", "s_fcT",
                             "s_fcT_cp", "s_pjT", "s_pjT_cp", "s_lnb", "s_ob", "s_ob_cp", "s_pjln"))

        def stage_sems(chain, names):
            return {n: sem(f"{chain}_{n}") for n in names.split()}

        NORM = "bn mv ve rstd xn xT_mm xT "
        A = stage_sems("A", NORM + "ctx s_mm sim mx p rs a aT_mm aT mxT_mm m4 m4d gm_mm gmax msh eb hc_mm erec hc "
                       "w14 hq_mm prod out_mm x")
        B = stage_sems("B", NORM + "shift s_mm uP uV sum acc xb out_mm x")
        C = stage_sems("C", NORM + "s_mm mx p rs a aT_mm aT out_mm x")
        Dd = stage_sems("D", NORM + "lo fc_mm gel bn2 mv2")
        E = stage_sems("E", "ve rstd shift gnA gnV gT_mm gT xe out_mm x")

        block = es.enter_context(nc.Block())

        passed = {e: sem(f"passed_{e}") for e in ("sp", "dve", "pool")}

        def wait_alone(name, eng, semaphore, value):
            eng.wait_ge(semaphore, value)
            eng.sem_inc(passed[name], 1)

        def is_first(g):
            return isinstance(g, int) and g == 0

        def before(eng, semaphore, g, per_group=1, n=0):
            if not isinstance(g, int) or g >= 1:
                eng.wait_ge(semaphore, per_group * g + n)

        def xg(g):
            return X[:, bass.ds(g * GC, GC)]

        def keys_of(t, g):
            return t[:, bass.ds(g * P, P)]

        def xtile(g, k):
            return X[:, bass.ds(g * GC + k * P, P)]

        def tiles(ap):
            return ap.rearrange("p (k d) -> p k d", k=GT)

        @block.sync
        def _(sp):
            def load_x(g):
                sp.dma_start(xg(g), x[bass.ds(2 * g, 2), :, :].rearrange("b (p t) d -> p b (t d)", t=2)).then_inc(ld_x, 16)

            def x_landed(g):
                wait_alone("sp", sp, ld_x, 16 * (g + 1))

            def load_keys(g):
                before(sp, A["hq_mm"], g)
                sp.dma_start(ctxA[:, :], ctx[bass.ds(2 * g, 2), :, :].rearrange("b k d -> (b k) d")).then_inc(A["ctx"], 16)

            sp.dma_start(CTX[:, :].rearrange("k (g d) -> k g d", g=NG),
                         ctx.rearrange("(g b) k d -> (b k) g d", b=2)).then_inc(ld_ctx, 16)
            load_x(0)
            sp.dma_start(wqv[:, :, :], W_qv.rearrange("(k p) n -> p k n", p=P)).then_inc(ld_qv, 16)
            sp.dma_start(bqv_rep[:, :], b_qv.rearrange("(a n) -> a n", a=1).to_broadcast([P, P])).then_inc(ld_keys, 16)
            sp.dma_start(bsim[:, :], b_sim.rearrange("(a n) -> a n", a=1).to_broadcast([P, 1])).then_inc(ld_keys, 16)
            load_keys(0)
            x_landed(0)
            load_x(1)
            for half in range(2):
                for src, dst in ((W1, w1_in), (b1, b1_in), (W2, w2_in)):
                    sp.dma_start(dst[half * M:(half + 1) * M, :], src[:, half * HALF:(half + 1) * HALF]).then_inc(ld_inner, 16)
            x_landed(1)
            with sp.Fori(2, NG) as g:
                load_x(g)
                x_landed(g)
            with sp.Fori(1, NG) as g:
                load_keys(g)

            def store(g):
                wait_alone("sp", sp, E["x"], g + 1)
                sp.dma_start(out[bass.ds(2 * g, 2), :, :].rearrange("b (p t) d -> p b (t d)", t=2), xg(g)).then_inc(stored, 16)

            with sp.Fori(0, NG) as g:
                store(g)
            sp.wait_ge(stored, 16 * NG)

        @block.gpsimd
        def _(pool):
            pool.memset(rows[:, :], 0.0).then_inc(s_rows0, 1)
            pool.memset(ident[:, :], 0.0).then_inc(s_id0, 1)
            pool.wait_ge(s_id0, 1)
            pool.affine_select(out=ident[:, :], in_=ident[:, :], compare_op=ALU.not_equal, fill=1.0,
                               base=0, pattern=[[-1, P]], channel_multiplier=1).then_inc(s_ident, 1)
            pool.memset(ones[:, :], 1.0).then_inc(s_ones, 1)
            pool.memset(neg_half[:, :], -0.5).then_inc(s_ones, 1)
            pool.memset(eps[:, :], EPS).then_inc(s_ones, 1)
            pool.dma_start(wk[:, :], WK).then_inc(ld_proj, 16)
            pool.dma_start(wq[:, :], WQ).then_inc(ld_proj, 16)
            pool.dma_start(wv[:, :], WV).then_inc(ld_proj, 16)
            pool.memset(aTA[:, :, :], 0.0).then_inc(s_zero, 1)
            pool.memset(aTC[:, :, :], 0.0).then_inc(s_zero, 1)

            def load_ffn_weights():
                for half in range(2):
                    pool.dma_start(win[:, half, :], Win).then_inc(ld_in, 16)
                    pool.dma_start(wout[half * M:(half + 1) * M, :], Wout).then_inc(ld_out, 16)
                pool.dma_start(bout_rep[:, :], bout.rearrange("(a n) -> a n", a=1).to_broadcast([P, P])).then_inc(ld_out, 16)
                pool.dma_start(wfc[:, :, :], W_fc.rearrange("(c p) d -> p c d", p=P)).then_inc(ld_ffn, 16)
                pool.dma_start(wpj[:, :, :], W_proj.rearrange("d (c h) -> d c h", c=HC)).then_inc(ld_ffn, 16)

            def rstd(ch, n, g):
                pool.wait_ge(ch["mv"], g + 1)
                pool.tensor_tensor(n["ve"][:, :], n["mv"][:, :, 1], eps[:, :], ALU.add).then_inc(ch["ve"], 1)
                pool.wait_ge(ch["ve"], g + 1)
                if ch is B:
                    before(pool, B["xn"], g)
                pool.tensor_tensor(n["rstd"][:, :], n["ve"][:, :], neg_half[:, :], ALU.pow).then_inc(ch["rstd"], 1)

            def normalise(ch, p, rs, a, g):
                pool.wait_ge(ch["rs"], g + 1)
                before(pool, ch["aT_mm"], g)
                pool.tensor_tensor(a[:, :, :].rearrange("p t (b j) -> p (t b) j", b=2),
                                   p[:, :, :].rearrange("p t (b j) -> p (t b) j", b=2),
                                   rs[:, :].unsqueeze(2).to_broadcast([P, 4, SK]), ALU.mult).then_inc(ch["a"], 1)

            def add_bout(g):
                if is_first(g):
                    pool.wait_ge(ld_out, 48)
                before(pool, B["x"], g)
                pool.wait_ge(A["x"], g + 1)
                pool.tensor_tensor(tiles(xb[:, :]), tiles(xg(g)),
                                   bout_rep[:, :].unsqueeze(1).to_broadcast([P, GT, P]), ALU.add).then_inc(B["xb"], 1)

            def add_out_bias(g):
                if is_first(g):
                    pool.wait_ge(s_ob_cp, 1)
                pool.wait_ge(C["x"], g + 1)
                before(pool, E["x"], g)
                pool.tensor_tensor(tiles(xe[:, :]), tiles(xg(g)),
                                   out_bias[:, :].unsqueeze(1).to_broadcast([P, GT, P]), ALU.add).then_inc(E["xe"], 1)

            def rstd_hidden(g):
                pool.wait_ge(Dd["mv2"], g + 1)
                pool.tensor_tensor(veE[:, :], mvE[:, :, 1], eps[:, :], ALU.add).then_inc(E["ve"], 1)
                pool.wait_ge(E["ve"], g + 1)
                before(pool, E["gnV"], g, NV)
                before(pool, E["gnA"], g, NA)
                pool.tensor_tensor(rsE[:, :], veE[:, :], neg_half[:, :], ALU.pow).then_inc(E["rstd"], 1)

            pool.wait_ge(s_ones, 3)

            rstd(A, nA, 0)
            load_ffn_weights()
            normalise(A, pA, rsA, aA, 0)
            rstd(A, nA, 1)
            rstd(B, nB, 0)
            normalise(A, pA, rsA, aA, 1)
            rstd(A, nA, 2)
            add_bout(0)
            rstd(B, nB, 1)
            normalise(A, pA, rsA, aA, 2)
            rstd(A, nA, 3)
            rstd(C, nC, 0)
            add_bout(1)
            rstd(B, nB, 2)
            normalise(C, pC, rsC, aC, 0)
            normalise(A, pA, rsA, aA, 3)
            rstd(C, nC, 1)
            with pool.Fori(K + 1, NG) as i:
                add_bout(i - 2)
                rstd(A, nA, i)
                rstd(B, nB, i - 1)
                normalise(C, pC, rsC, aC, i - 3)
                normalise(A, pA, rsA, aA, i)
                rstd(C, nC, i - 2)
            rstd(Dd, nD, 0)
            add_bout(6)
            rstd(Dd, nD, 1)
            rstd(B, nB, 7)
            normalise(C, pC, rsC, aC, 5)
            add_bout(7)
            rstd_hidden(0)
            rstd(C, nC, 6)
            rstd(Dd, nD, 2)
            add_out_bias(0)
            rstd_hidden(1)
            normalise(C, pC, rsC, aC, 6)
            rstd(C, nC, 7)
            rstd(Dd, nD, 3)
            normalise(C, pC, rsC, aC, 7)
            with pool.Fori(K2 + 1, NG) as i:
                add_out_bias(i - 3)
                rstd_hidden(i - 2)
                rstd(Dd, nD, i)
            rstd_hidden(6)
            add_out_bias(5)
            add_out_bias(6)
            rstd_hidden(7)
            add_out_bias(7)

        @block.scalar
        def _(act):
            act.wait_ge(s_rows0, 1)
            act.dma_start(rows[0:3, :], w_sim.rearrange("(a n) -> a n", a=3)).then_inc(ld_rows, 16)
            act.dma_start(rows[3:7, :], ln_w.rearrange("(a n) -> a n", a=HC)).then_inc(ld_rows, 16)
            act.dma_start(rows[7:11, :], ln_b.rearrange("(a n) -> a n", a=HC)).then_inc(ld_rows, 16)
            act.dma_start(rows[11:12, 0:M], b2.rearrange("(a n) -> a n", a=1)).then_inc(ld_rows, 16)
            for half in range(2):
                act.dma_start(rows[12:13, half * M:(half + 1) * M], bin_.rearrange("(a n) -> a n", a=1)).then_inc(ld_rows, 16)

            def weight_columns():
                act.wait_ge(s_rowsT, 1)
                act.activation(cols[:, :], bank[6][:, 0:13], ACT.Copy).then_inc(s_cols, 1)

            def keys_transposed():
                for half in range(2):
                    act.wait_ge(s_cT_mm, half + 1)
                    act.activation(cT[:, half * 512:(half + 1) * 512], bank[4 + half][:, :], ACT.Copy).then_inc(s_cT, 1)

            def key_weights():
                act.wait_ge(s_wk_mm, 1)
                act.activation(wkq[:, :], bank[7][:, 0:P], ACT.Copy, scale=SCALE).then_inc(s_wk, 1)
                act.activation(wvT[:, :], bank[7][:, P:2 * P], ACT.Copy).then_inc(s_wk, 1)

            def keys_by_w2():
                act.wait_ge(ld_keys, 32)
                for half, src in enumerate((bank[6], bank[1])):
                    act.wait_ge(s_rkey_mm, half + 1)
                    act.activation(rkey[:, half * 512:(half + 1) * 512], src[:, :], ACT.Identity, bias=bsim[:, 0:1]).then_inc(s_rkey, 1)

            def projected_keys():
                for half, src in enumerate((bank[1], bank[3])):
                    act.wait_ge(s_proj_mm, half + 1)
                    act.activation(projkey[:, half * 512:(half + 1) * 512], src[:, :], ACT.Copy).then_inc(s_proj, 1)

            def key_values():
                for half, src in enumerate((bank[5], bank[6])):
                    act.wait_ge(s_val_mm, half + 1)
                    act.activation(values[:, half * 512:(half + 1) * 512], src[:, :], ACT.Copy).then_inc(s_val, 1)

            def evac_xT(ch, src, dst, g):
                act.wait_ge(ch["xT_mm"], g + 1)
                before(act, (B["s_mm"] if ch is B else ch["out_mm"]), g)
                act.activation(dst[:, :], src[:, :], ACT.Copy).then_inc(ch["xT"], 1)

            def exps(ch, sc, mx, p, sm, g):
                act.wait_ge(ch["mx"], g + 1)
                before(act, ch["a"], g)
                for t in range(2):
                    for b in range(2):
                        q = 2 * t + b
                        last = act.activation(p[:, t, b * SK:(b + 1) * SK], sc[:, t, b * SK:(b + 1) * SK], ACT.Exp,
                                              bias=mx[:, q:q + 1], accum_out=sm[:, q:q + 1])
                last.then_inc(ch["p"], 1)

            def evac_aT(ch, src, dst, g):
                if is_first(g):
                    act.wait_ge(s_zero, 2)
                """each batch's weights to their own copy; the other batch's partitions stay zero"""
                act.wait_ge(ch["aT_mm"], g + 1)
                before(act, ch["out_mm"], g)
                for b in range(2):
                    rows_b = slice(b * SK, (b + 1) * SK)
                    last = act.activation(dst[rows_b, b, :], src[rows_b, 0:2 * P], ACT.Copy)
                last.then_inc(ch["aT"], 1)

            def batch_exps(g):
                act.wait_ge(A["msh"], g + 1)
                act.activation(eb[:, :], msh[:, :], ACT.Exp).then_inc(A["eb"], 1)

            def norm_rows(g):
                act.wait_ge(B["shift"], g + 1)
                before(act, B["xT_mm"], g)
                for k in range(GT):
                    last = act.activation(nB["xn"][:, k * P:(k + 1) * P], xtile(g, k), ACT.Identity,
                                          bias=shiftB[:, k:k + 1], scale=nB["rstd"][:, k:k + 1])
                last.then_inc(B["xn"], 1)

            def units(g, k):
                if is_first(g):
                    act.wait_ge(s_b1s, 1)
                """a pair of hidden units of the inner mlp, for all tokens"""
                act.wait_ge(B["s_mm"], g + 1)
                if k < KP:
                    before(act, B["sum"], g, KP, k + 1 - KP)
                else:
                    before(act, B["acc"], g, KV, k - KP + 1 - KV)
                act.activation(u[:, k, :], bank[5][:, :], ACT.Relu, bias=b1_s[:, k:k + 1],
                               scale=w1_in[:, k:k + 1]).then_inc(B["uP"] if k < KP else B["uV"], 1)

            def up_weights():
                act.wait_ge(s_fcT, 1)
                act.activation(wfcT[:, :], bank[6][:, :], ACT.Copy).then_inc(s_fcT_cp, 1)

            def down_weights():
                act.wait_ge(s_pjT, 1)
                act.activation(wpjT[:, :, :].rearrange("p c d -> p (c d)"), bank[5][:, :], ACT.Copy).then_inc(s_pjT_cp, 1)

            def out_bias_row():
                act.wait_ge(s_ob, 1)
                act.activation(out_bias[:, :], bank[6][:, 0:P], ACT.Copy).then_inc(s_ob_cp, 1)

            def high_half(g):
                act.wait_ge(Dd["xT_mm"], g + 1)
                before(act, Dd["fc_mm"], g, GT)
                act.activation(hiD[:, :], bank[2][:, :], ACT.Copy).then_inc(Dd["xT"], 1)

            def gelu(g, k):
                act.wait_ge(Dd["fc_mm"], GT * g + k + 1)
                if k in DVE_TILES:
                    before(act, E["gnV"], g, NV, DVE_TILES.index(k) + 1 - NV)
                else:
                    before(act, E["gnA"], g, NA, ACT_TILES.index(k) + 1 - NA)
                act.activation(gel[:, k, :], bank[2 + 2 * (k % 2)][:, :], ACT.Gelu).then_inc(Dd["gel"], 1)

            def hidden_norm(g, k):
                act.wait_ge(E["shift"], g + 1)
                before(act, E["gT_mm"], g, GT, k + 1 - GT)
                act.activation(gn[:, k, :], gel[:, k, :], ACT.Identity, bias=shiftE[:, k:k + 1],
                               scale=rsE[:, k:k + 1]).then_inc(E["gnA"], 1)

            def evac_gT(g, k):
                act.wait_ge(E["gT_mm"], GT * g + k + 1)
                before(act, E["out_mm"], g, GT, k + 1 - GT)
                act.activation(gnT[:, k, :], bank[0][:, :], ACT.Copy).then_inc(E["gT"], 1)

            keys_transposed()
            weight_columns()
            key_weights()
            evac_xT(A, bank[0], xTA, 0)
            keys_by_w2()
            exps(A, simA, mxA, pA, smA, 0)
            batch_exps(0)
            key_values()
            evac_aT(A, bank[2], aTA, 0)
            evac_xT(A, bank[0], xTA, 1)
            up_weights()
            down_weights()
            exps(A, simA, mxA, pA, smA, 1)
            projected_keys()
            batch_exps(1)
            norm_rows(0)
            evac_aT(A, bank[2], aTA, 1)
            out_bias_row()
            evac_xT(B, bank[5], xTB, 0)
            units(0, KP + 0)
            units(0, 0)
            units(0, KP + 1)
            units(0, 1)
            units(0, KP + 2)
            evac_xT(A, bank[0], xTA, 2)
            units(0, 2)
            units(0, KP + 3)
            units(0, 3)
            exps(A, simA, mxA, pA, smA, 2)
            batch_exps(2)
            norm_rows(1)
            evac_aT(A, bank[2], aTA, 2)
            evac_xT(B, bank[5], xTB, 1)
            units(1, KP + 0)
            units(1, 0)
            units(1, KP + 1)
            units(1, 1)
            units(1, KP + 2)
            evac_xT(A, bank[0], xTA, 3)
            evac_xT(C, bank[1], xTC, 0)
            units(1, 2)
            units(1, KP + 3)
            units(1, 3)
            exps(C, scoresC, mxC, pC, smC, 0)
            exps(A, simA, mxA, pA, smA, 3)
            batch_exps(3)
            evac_aT(C, bank[3], aTC, 0)
            norm_rows(2)
            evac_aT(A, bank[2], aTA, 3)
            evac_xT(B, bank[5], xTB, 2)
            with act.Fori(K + 1, NG) as i:
                units(i - 2, KP + 0)
                units(i - 2, 0)
                units(i - 2, KP + 1)
                units(i - 2, 1)
                evac_xT(C, bank[1], xTC, i - 3)
                evac_xT(A, bank[0], xTA, i)
                units(i - 2, KP + 2)
                units(i - 2, 2)
                units(i - 2, KP + 3)
                units(i - 2, 3)
                exps(C, scoresC, mxC, pC, smC, i - 3)
                exps(A, simA, mxA, pA, smA, i)
                batch_exps(i)
                evac_aT(C, bank[3], aTC, i - 3)
                norm_rows(i - 1)
                evac_aT(A, bank[2], aTA, i)
                evac_xT(B, bank[5], xTB, i - 1)
            units(6, KP + 0)
            units(6, 0)
            units(6, KP + 1)
            units(6, 1)
            units(6, KP + 2)
            evac_xT(C, bank[1], xTC, 5)
            units(6, 2)
            high_half(0)
            units(6, KP + 3)
            units(6, 3)
            exps(C, scoresC, mxC, pC, smC, 5)
            gelu(0, 0)
            gelu(0, 1)
            norm_rows(7)
            gelu(0, 2)
            gelu(0, 3)
            evac_xT(B, bank[5], xTB, 7)
            evac_aT(C, bank[3], aTC, 5)
            high_half(1)
            units(7, KP + 0)
            units(7, 0)
            units(7, KP + 1)
            units(7, 1)
            units(7, KP + 2)
            gelu(1, 0)
            hidden_norm(0, 1)
            units(7, 2)
            hidden_norm(0, 3)
            evac_gT(0, 0)
            gelu(1, 1)
            evac_xT(C, bank[1], xTC, 6)
            units(7, KP + 3)
            units(7, 3)
            gelu(1, 2)
            gelu(1, 3)
            evac_gT(0, 1)
            exps(C, scoresC, mxC, pC, smC, 6)
            evac_gT(0, 2)
            high_half(2)
            hidden_norm(1, 1)
            evac_aT(C, bank[3], aTC, 6)
            evac_gT(0, 3)
            gelu(2, 0)
            gelu(2, 1)
            evac_xT(C, bank[1], xTC, 7)
            hidden_norm(1, 3)
            evac_gT(1, 0)
            gelu(2, 2)
            exps(C, scoresC, mxC, pC, smC, 7)
            gelu(2, 3)
            evac_aT(C, bank[3], aTC, 7)
            evac_gT(1, 1)
            high_half(3)
            with act.Fori(K2 + 1, NG) as i:
                evac_gT(i - 3, 2)
                evac_gT(i - 3, 3)
                hidden_norm(i - 2, 1)
                hidden_norm(i - 2, 3)
                gelu(i - 1, 0)
                gelu(i - 1, 1)
                evac_gT(i - 2, 0)
                gelu(i - 1, 2)
                gelu(i - 1, 3)
                evac_gT(i - 2, 1)
                high_half(i)
            evac_gT(5, 2)
            evac_gT(5, 3)
            hidden_norm(6, 1)
            gelu(7, 0)
            evac_gT(6, 0)
            gelu(7, 1)
            gelu(7, 2)
            evac_gT(6, 1)
            hidden_norm(6, 3)
            gelu(7, 3)
            evac_gT(6, 2)
            evac_gT(6, 3)
            hidden_norm(7, 1)
            evac_gT(7, 0)
            evac_gT(7, 1)
            hidden_norm(7, 3)
            evac_gT(7, 2)
            evac_gT(7, 3)

        @block.vector
        def _(dve):
            def stats(ch, n, g):
                before(dve, ch["mv"], g)
                if ch is A:
                    wait_alone("dve", dve, ld_x, 16 * (g + 1))
                else:
                    wait_alone("dve", dve, (A if ch is B else B if ch is C else C)["x"], g + 1)
                for k in range(GT):
                    dve.bn_stats(n["stats"][:, k, :], xtile(g, k)).then_inc(ch["bn"], 1)

            def aggregate(ch, n, g):
                before(dve, B["shift"] if ch is B else ch["xn"], g)
                wait_alone("dve", dve, ch["bn"], GT * (g + 1))
                for k in range(GT):
                    last = dve.bn_aggr(n["mv"][:, k, :], n["stats"][:, k, :])
                last.then_inc(ch["mv"], 1)

            def norm(ch, n, g):
                dve.wait_ge(ch["rstd"], g + 1)
                before(dve, A["hc_mm"] if ch is A else ch["xT_mm"], g)
                for k in range(GT):
                    last = dve.tensor_scalar(n["xn"][:, k * P:(k + 1) * P], xtile(g, k), n["mv"][:, k, 0:1],
                                             n["rstd"][:, k:k + 1], ALU.subtract, ALU.mult)
                last.then_inc(ch["xn"], 1)

            def norm_shift(g):
                dve.wait_ge(B["rstd"], g + 1)
                before(dve, B["xn"], g)
                dve.scalar_tensor_tensor(shiftB[:, :], nB["mv"][:, :, 0], -1.0, nB["rstd"][:, :], ALU.mult, ALU.mult)\
                    .then_inc(B["shift"], 1)

            def key_term(g):
                if is_first(g):
                    dve.wait_ge(s_rkey, 2)
                dve.wait_ge(A["s_mm"], g + 1)
                before(dve, A["p"], g)
                dve.tensor_tensor(simA[:, :, :], bank[2][:, 0:2 * P].rearrange("p (t n) -> p t n", t=2),
                                  keys_of(rkey, g).unsqueeze(1).to_broadcast([P, 2, P]), ALU.add).then_inc(A["sim"], 1)

            def row_max(ch, sc, mx, g):
                dve.wait_ge(ch["sim"] if ch is A else ch["s_mm"], g + 1)
                before(dve, ch["mxT_mm"] if ch is A else ch["p"], g)
                dve.tensor_reduce(mx[:, :], sc[:, :, :].rearrange("p t (b j) -> p (t b) j", b=2), AX_X, ALU.max,
                                  negate=True).then_inc(ch["mx"], 1)

            def row_scale(ch, sm, rs, g):
                dve.wait_ge(ch["p"], g + 1)
                dve.reciprocal(rs[:, :], sm[:, :]).then_inc(ch["rs"], 1)

            def tile_max(g):
                dve.wait_ge(A["mxT_mm"], g + 1)
                dve.tensor_reduce(m4[:, :], bank[4][0:4, 0:P], AX_X, ALU.min).then_inc(A["m4"], 1)

            def tile_max_diagonal(g):
                dve.wait_ge(A["m4"], g + 1)
                dve.tensor_scalar(m4d[:, :], ident[0:4, 0:4], m4[:, 0:1], None, ALU.mult).then_inc(A["m4d"], 1)

            def batch_max(g):
                dve.wait_ge(A["gm_mm"], g + 1)
                dve.tensor_reduce(gmax[:, :], bank[4][:, P:P + 4].rearrange("p (t b) -> p b t", b=2), AX_X,
                                  ALU.min).then_inc(A["gmax"], 1)

            def batch_shift(g):
                dve.wait_ge(A["gmax"], g + 1)
                dve.tensor_tensor(msh[:, :].rearrange("p (t b) -> p t b", b=2),
                                  gmax[:, :].unsqueeze(1).to_broadcast([P, 2, 2]),
                                  mxA[:, :].rearrange("p (t b) -> p t b", b=2), ALU.subtract).then_inc(A["msh"], 1)

            def batch_scale(g):
                dve.wait_ge(A["hc_mm"], g + 1)
                dve.reciprocal(erec[:, :], bank[4][:, P + 4:P + 6]).then_inc(A["erec"], 1)

            def batch_mean(g):
                dve.wait_ge(A["erec"], g + 1)
                dve.tensor_tensor(hc[:, :], bank[4][:, P + 8:P + 10], erec[:, :], ALU.mult).then_inc(A["hc"], 1)

            def fold_mean(g):
                if is_first(g):
                    dve.wait_ge(ld_qv, 16)
                """one weight matrix for the two terms that are linear in the normalised x"""
                dve.wait_ge(A["hc"], g + 1)
                before(dve, A["out_mm"], g)
                for b in range(2):
                    last = dve.scalar_tensor_tensor(w14[:, b, :], wqv[:, 3, :], hc[:, b:b + 1], wqv[:, 0, :],
                                                    ALU.mult, ALU.add)
                last.then_inc(A["w14"], 1)

            def product(g):
                dve.wait_ge(A["hq_mm"], g + 1)
                before(dve, A["out_mm"], g)
                dve.tensor_tensor(prodT[:, :], bank[4][:, :], xTA[:, :], ALU.mult).then_inc(A["prod"], 1)

            def sum_pair(g, k):
                if is_first(g) and k == 0:
                    dve.wait_ge(s_b1, 1)
                """VectorE's share of the inner mlp's second layer"""
                dve.wait_ge(B["uV"], KV * g + k + 1)
                w = w2_in[:, KP + k:KP + k + 1]
                if k == 0:
                    before(dve, B["out_mm"], g)
                    dve.tensor_scalar(acc[:, :], u[:, KP, :], w, b2_half[:, 0:1], ALU.mult, ALU.add).then_inc(B["acc"], 1)
                else:
                    dve.wait_ge(B["acc"], KV * g + k)
                    dve.scalar_tensor_tensor(acc[:, :], u[:, KP + k, :], w, acc[:, :], ALU.mult, ALU.add).then_inc(B["acc"], 1)

            def residual(ch, g):
                dve.wait_ge(ch["out_mm"], g + 1)
                dve.tensor_tensor(xg(g), bank[7 if ch is A else 1][:, :], xg(g), ALU.add).then_inc(ch["x"], 1)

            def residual_ffn(g):
                dve.wait_ge(B["out_mm"], g + 1)
                dve.wait_ge(B["xb"], g + 1)
                dve.tensor_tensor(xg(g), bank[6][:, :], xb[:, :], ALU.add).then_inc(B["x"], 1)

            def spread_w2():
                dve.wait_ge(s_cols, 1)
                dve.wait_ge(s_ones, 1)
                dve.tensor_scalar(w2_rep[:, :], ones[:, :], w2_sim, None, ALU.mult).then_inc(s_w2rep, 1)

            def similarity_keys():
                dve.wait_ge(s_cT, 2)
                dve.wait_ge(s_cols, 1)
                dve.tensor_scalar(simkey[:, :], cT[:, :], w3_sim, w1_sim, ALU.mult, ALU.add).then_inc(s_simkey, 1)

            def key_outputs():
                dve.wait_ge(ld_keys, 32)
                for half, src in enumerate((bank[3], bank[5])):
                    dve.wait_ge(s_cw2_mm, half + 1)
                    dve.tensor_tensor(tiles(cw2[:, half * 512:(half + 1) * 512]), tiles(src[:, :]),
                                      bqv_rep[:, :].unsqueeze(1).to_broadcast([P, 4, P]), ALU.add).then_inc(s_cw2, 1)

            def unit_biases():
                dve.wait_ge(ld_inner, 96)
                dve.wait_ge(s_cols, 1)
                dve.scalar_tensor_tensor(b1_s[:, :], w1_in[:, :], bin_col, b1_in[:, :], ALU.mult, ALU.add).then_inc(s_b1s, 1)
                dve.tensor_scalar(b2_half[:, :], b2_col, 1.0, None, ALU.mult).then_inc(s_b1, 1)

            def folded_output():
                dve.wait_ge(ld_out, 48)
                for k in range(KP):
                    dve.tensor_scalar(wsum[:, k, :], wout[:, :], w2_in[:, k:k + 1], None, ALU.mult).then_inc(s_wsum, 1)

            def weight_sums():
                dve.wait_ge(ld_ffn, 32)
                for k, w in enumerate((wfc, wpj)):
                    dve.tensor_reduce(absum[:, k:k + 1], w[:, :, :].rearrange("p c d -> p (c d)"), AX_X, ALU.add,
                                      apply_absolute_value=True).then_inc(s_absum, 1)

            def weight_scales():
                dve.wait_ge(s_absum_mm, 1)
                dve.tensor_scalar(gamma[:, :], bank[6][:, 16:18], 1.0 / (HID * D), ABSMEAN_EPS, ALU.mult, ALU.add).then_inc(s_gamma, 1)
                dve.wait_ge(s_gamma, 1)
                dve.reciprocal(inv_gamma[:, :], gamma[:, :]).then_inc(s_igamma, 1)

            def quantise(k):
                flat = (wfc, wpj)[k][:, :, :].rearrange("p c d -> p (c d)")
                dve.wait_ge(s_igamma, 1)
                dve.tensor_scalar(above[:, k, :], flat, inv_gamma[:, k:k + 1], 0.5, ALU.mult, ALU.is_gt).then_inc(s_above, 1)
                dve.tensor_scalar(below[:, k, :], flat, inv_gamma[:, k:k + 1], -0.5, ALU.mult, ALU.is_lt).then_inc(s_above, 1)
                dve.wait_ge(s_above, 2 * (k + 1))
                dve.tensor_tensor(flat, above[:, k, :], below[:, k, :], ALU.subtract).then_inc(s_quant, 1)

            def spread_norm_bias():
                for c in range(HC):
                    dve.tensor_scalar(lnb_rep[:, c, :], ones[:, :], lnb_col[c], None, ALU.mult).then_inc(s_lnb, 1)

            def fold_norm_weight():
                dve.wait_ge(s_pjT_cp, 1)
                for c in range(HC):
                    dve.tensor_scalar(wpjT_ln[:, c, :], wpjT[:, c, :], lnw_col[c], None, ALU.mult).then_inc(s_pjln, 1)

            def low_half(g):
                dve.wait_ge(Dd["xT"], g + 1)
                dve.tensor_tensor(loD[:, :], bank[2][:, :], hiD[:, :], ALU.subtract).then_inc(Dd["lo"], 1)

            def hidden_stats(g, k):
                wait_alone("dve", dve, Dd["gel"], GT * g + k + 1)
                dve.bn_stats(statsE[:, k, :], gel[:, k, :]).then_inc(Dd["bn2"], 1)

            def hidden_aggr(g):
                before(dve, E["gnV"], g, NV)
                before(dve, E["shift"], g)
                wait_alone("dve", dve, Dd["bn2"], GT * (g + 1))
                for k in range(GT):
                    last = dve.bn_aggr(mvE[:, k, :], statsE[:, k, :])
                last.then_inc(Dd["mv2"], 1)

            def hidden_shift(g):
                dve.wait_ge(E["rstd"], g + 1)
                dve.scalar_tensor_tensor(shiftE[:, :], mvE[:, :, 0], -1.0, rsE[:, :], ALU.mult, ALU.mult).then_inc(E["shift"], 1)

            def hidden_norm(g, k):
                dve.wait_ge(E["rstd"], g + 1)
                before(dve, E["gT_mm"], g, GT, k + 1 - GT)
                dve.tensor_scalar(gn[:, k, :], gel[:, k, :], mvE[:, k, 0:1], rsE[:, k:k + 1],
                                  ALU.subtract, ALU.mult).then_inc(E["gnV"], 1)

            def residual_out(g):
                dve.wait_ge(E["out_mm"], GT * (g + 1))
                dve.wait_ge(E["xe"], g + 1)
                dve.tensor_tensor(xg(g), bank[7][:, :], xe[:, :], ALU.add).then_inc(E["x"], 1)

            stats(A, nA, 0)
            aggregate(A, nA, 0)
            spread_w2()
            similarity_keys()
            norm(A, nA, 0)
            spread_norm_bias()
            key_outputs()
            stats(A, nA, 1)
            key_term(0)
            aggregate(A, nA, 1)
            row_max(A, simA, mxA, 0)
            stats(A, nA, 2)
            tile_max(0)
            tile_max_diagonal(0)
            row_scale(A, smA, rsA, 0)
            batch_max(0)
            batch_shift(0)
            weight_sums()
            unit_biases()
            batch_scale(0)
            weight_scales()
            batch_mean(0)
            norm(A, nA, 1)
            fold_mean(0)
            product(0)
            quantise(0)
            quantise(1)
            residual(A, 0)
            stats(B, nB, 0)
            key_term(1)
            row_max(A, simA, mxA, 1)
            aggregate(B, nB, 0)
            aggregate(A, nA, 2)
            tile_max(1)
            tile_max_diagonal(1)
            row_scale(A, smA, rsA, 1)
            batch_max(1)
            batch_shift(1)
            norm_shift(0)
            folded_output()
            batch_scale(1)
            batch_mean(1)
            fold_norm_weight()
            fold_mean(1)
            product(1)
            norm(A, nA, 2)
            sum_pair(0, 0)
            stats(A, nA, 3)
            sum_pair(0, 1)
            residual(A, 1)
            sum_pair(0, 2)
            stats(B, nB, 1)
            key_term(2)
            aggregate(B, nB, 1)
            row_max(A, simA, mxA, 2)
            sum_pair(0, 3)
            tile_max(2)
            tile_max_diagonal(2)
            row_scale(A, smA, rsA, 2)
            norm_shift(1)
            batch_max(2)
            batch_shift(2)
            aggregate(A, nA, 3)
            residual_ffn(0)
            stats(C, nC, 0)
            batch_scale(2)
            batch_mean(2)
            fold_mean(2)
            product(2)
            aggregate(C, nC, 0)
            norm(A, nA, 3)
            sum_pair(1, 0)
            norm(C, nC, 0)
            residual(A, 2)
            sum_pair(1, 1)
            stats(B, nB, 2)
            sum_pair(1, 2)
            aggregate(B, nB, 2)
            key_term(3)
            row_max(C, scoresC, mxC, 0)
            row_max(A, simA, mxA, 3)
            sum_pair(1, 3)
            tile_max(3)
            tile_max_diagonal(3)
            row_scale(C, smC, rsC, 0)
            batch_max(3)
            batch_shift(3)
            residual_ffn(1)
            row_scale(A, smA, rsA, 3)
            norm_shift(2)
            stats(C, nC, 1)
            batch_scale(3)
            aggregate(C, nC, 1)
            batch_mean(3)
            residual(C, 0)
            fold_mean(3)
            with dve.Fori(K + 1, NG) as i:
                stats(A, nA, i)
                product(i - 1)
                aggregate(A, nA, i)
                norm(C, nC, i - 3)
                sum_pair(i - 2, 0)
                norm(A, nA, i)
                sum_pair(i - 2, 1)
                residual(A, i - 1)
                stats(B, nB, i - 1)
                row_max(C, scoresC, mxC, i - 3)
                key_term(i)
                sum_pair(i - 2, 2)
                row_max(A, simA, mxA, i)
                aggregate(B, nB, i - 1)
                sum_pair(i - 2, 3)
                tile_max(i)
                tile_max_diagonal(i)
                row_scale(C, smC, rsC, i - 3)
                batch_max(i)
                norm_shift(i - 1)
                batch_shift(i)
                row_scale(A, smA, rsA, i)
                residual_ffn(i - 2)
                stats(C, nC, i - 2)
                batch_scale(i)
                aggregate(C, nC, i - 2)
                batch_mean(i)
                residual(C, i - 3)
                fold_mean(i)
            stats(Dd, nD, 0)
            product(7)
            aggregate(Dd, nD, 0)
            norm(C, nC, 5)
            stats(Dd, nD, 1)
            norm(Dd, nD, 0)
            sum_pair(6, 0)
            residual(A, 7)
            aggregate(Dd, nD, 1)
            stats(B, nB, 7)
            row_max(C, scoresC, mxC, 5)
            aggregate(B, nB, 7)
            low_half(0)
            sum_pair(6, 1)
            norm(Dd, nD, 1)
            sum_pair(6, 2)
            row_scale(C, smC, rsC, 5)
            norm_shift(7)
            sum_pair(6, 3)
            stats(Dd, nD, 2)
            hidden_stats(0, 0)
            hidden_stats(0, 1)
            residual_ffn(6)
            hidden_stats(0, 2)
            hidden_stats(0, 3)
            aggregate(Dd, nD, 2)
            hidden_aggr(0)
            stats(C, nC, 6)
            low_half(1)
            aggregate(C, nC, 6)
            hidden_norm(0, 0)
            sum_pair(7, 0)
            hidden_shift(0)
            residual(C, 5)
            norm(C, nC, 6)
            hidden_stats(1, 0)
            sum_pair(7, 1)
            hidden_norm(0, 2)
            norm(Dd, nD, 2)
            sum_pair(7, 2)
            hidden_stats(1, 1)
            sum_pair(7, 3)
            row_max(C, scoresC, mxC, 6)
            hidden_stats(1, 2)
            hidden_stats(1, 3)
            residual_ffn(7)
            hidden_aggr(1)
            stats(C, nC, 7)
            row_scale(C, smC, rsC, 6)
            aggregate(C, nC, 7)
            hidden_shift(1)
            low_half(2)
            hidden_norm(1, 0)
            norm(C, nC, 7)
            residual(C, 6)
            stats(Dd, nD, 3)
            hidden_norm(1, 2)
            aggregate(Dd, nD, 3)
            hidden_stats(2, 0)
            row_max(C, scoresC, mxC, 7)
            hidden_stats(2, 1)
            residual_out(0)
            hidden_stats(2, 2)
            row_scale(C, smC, rsC, 7)
            norm(Dd, nD, 3)
            hidden_stats(2, 3)
            hidden_aggr(2)
            residual(C, 7)
            with dve.Fori(K2 + 1, NG) as i:
                stats(Dd, nD, i)
                low_half(i - 1)
                aggregate(Dd, nD, i)
                hidden_shift(i - 2)
                hidden_norm(i - 2, 0)
                hidden_norm(i - 2, 2)
                residual_out(i - 3)
                norm(Dd, nD, i)
                hidden_stats(i - 1, 0)
                hidden_stats(i - 1, 1)
                hidden_stats(i - 1, 2)
                hidden_stats(i - 1, 3)
                hidden_aggr(i - 1)
            low_half(7)
            hidden_shift(6)
            hidden_norm(6, 0)
            hidden_norm(6, 2)
            hidden_stats(7, 0)
            hidden_stats(7, 1)
            residual_out(5)
            hidden_stats(7, 2)
            hidden_stats(7, 3)
            hidden_aggr(7)
            hidden_shift(7)
            hidden_norm(7, 0)
            hidden_norm(7, 2)
            residual_out(6)
            residual_out(7)

        @block.tensor
        def _(pe):
            def xT(ch, n, dst, g):
                pe.wait_ge(ch["xn"], g + 1)
                if ch is A:
                    before(pe, A["xT"], g)
                elif ch is B:
                    if is_first(g):
                        pe.wait_ge(s_pjT_cp, 1)
                        pe.wait_ge(s_val, 2)
                    before(pe, B["uP"], g, KP)
                    before(pe, B["uV"], g, KV)
                elif ch is C:
                    if is_first(g):
                        pe.wait_ge(s_proj, 2)
                    before(pe, C["x"], g)
                else:
                    if is_first(g):
                        pe.wait_ge(A["aT"], NG)
                    before(pe, Dd["gel"], g, GT, 3 - GT)
                for k in range(GT):
                    last = pe.transpose(dst[:, k * P:(k + 1) * P], n["xn"][:, k * P:(k + 1) * P], ident[:, :])
                last.then_inc(ch["xT_mm"], 1)

            def scores(ch, xt, keys, dst, g):
                if is_first(g):
                    if ch is A:
                        pe.wait_ge(s_simkey, 1)
                    else:
                        pe.wait_ge(s_proj, 2)
                pe.wait_ge(ch["xT"], g + 1)
                before(pe, ch["aT"], g)
                for t in range(2):
                    for b in range(2):
                        k = 2 * b + t
                        last = pe.matmul(dst[:, t * P + b * SK:t * P + (b + 1) * SK], xt[:, k * P:(k + 1) * P],
                                         keys[:, bass.ds(g * P + b * SK, SK)], start=True, stop=True)
                last.then_inc(ch["s_mm"], 1)

            def aT(ch, a, dst, g):
                pe.wait_ge(ch["a"], g + 1)
                for t in range(2):
                    last = pe.transpose(dst[:, t * P:(t + 1) * P], a[:, t, :], ident[:, :])
                last.then_inc(ch["aT_mm"], 1)

            def turn_max(g):
                if is_first(g):
                    pe.wait_ge(s_cT, 1)
                pe.wait_ge(A["mx"], g + 1)
                before(pe, A["prod"], g)
                pe.transpose(bank[4][0:4, 0:P], mxA[:, :], ident[:, :]).then_inc(A["mxT_mm"], 1)

            def spread_max(g):
                pe.wait_ge(A["m4d"], g + 1)
                pe.matmul(bank[4][:, P:P + 4], ones[0:4, :], m4d[:, :], start=True, stop=True).then_inc(A["gm_mm"], 1)

            def batch_sums(g):
                pe.wait_ge(A["eb"], g + 1)
                for t in range(2):
                    pe.matmul(bank[4][:, P + 4:P + 6], ones[:, :], eb[:, 2 * t:2 * t + 2], start=(t == 0), stop=(t == 1))
                for b in range(2):
                    for t in range(2):
                        k = 2 * b + t
                        last = pe.matmul(bank[4][:, P + 8 + b:P + 9 + b], nA["xn"][:, k * P:(k + 1) * P],
                                         eb[:, 2 * t + b:2 * t + b + 1], start=(t == 0), stop=(t == 1))
                last.then_inc(A["hc_mm"], 1)

            def attended(g):
                pe.wait_ge(A["aT"], g + 1)
                pe.wait_ge(A["hc"], g + 1)
                pe.wait_ge(A["ctx"], 16 * (g + 1))
                for b in range(2):
                    last = pe.matmul(bank[4][:, b * 2 * P:(b + 1) * 2 * P], ctxA[:, :], aTA[:, b, :], start=True, stop=True)
                last.then_inc(A["hq_mm"], 1)

            def outA(g, k):
                b, t = k // 2, k % 2
                if k == 0:
                    if is_first(g):
                        pe.wait_ge(s_cw2, 2)
                        pe.wait_ge(s_wk, 2)
                    pe.wait_ge(A["prod"], g + 1)
                    pe.wait_ge(A["w14"], g + 1)
                    before(pe, A["x"], g)
                o = bank[7][:, k * P:(k + 1) * P]
                pe.matmul(o, aTA[:, b, t * P:(t + 1) * P], keys_of(cw2, g), start=True, stop=False)
                pe.matmul(o, xTA[:, k * P:(k + 1) * P], w14[:, b, :], start=False, stop=False)
                last = pe.matmul(o, prodT[:, k * P:(k + 1) * P], wqv[:, 2, :], start=False, stop=True)
                if k == GT - 1:
                    last.then_inc(A["out_mm"], 1)

            def inner(g):
                if is_first(g):
                    pe.wait_ge(ld_in, 32)
                pe.wait_ge(B["xT"], g + 1)
                pe.matmul(bank[5][:, :], win[:, :, :].rearrange("p a m -> p (a m)"), xTB[:, :], start=True, stop=True)\
                    .then_inc(B["s_mm"], 1)

            def sum_units(g, k):
                pe.wait_ge(B["uP"], KP * g + k + 1)
                if k == 0:
                    before(pe, B["x"], g)
                    if is_first(g):
                        pe.wait_ge(s_ob_cp, 1)
                        pe.wait_ge(s_wsum, KP)
                        pe.wait_ge(ld_out, 48)
                for j in range(GT):
                    last = pe.matmul(bank[6][:, j * P:(j + 1) * P], u[:, k, j * P:(j + 1) * P], wsum[:, k, :],
                                     start=(k == 0 and j == 0), stop=False, skip_group_check=True)
                last.then_inc(B["sum"], 1)

            def outB(g):
                pe.wait_ge(B["acc"], KV * (g + 1))
                for j in range(GT):
                    last = pe.matmul(bank[6][:, j * P:(j + 1) * P], acc[:, j * P:(j + 1) * P], wout[:, :],
                                     start=False, stop=True, skip_group_check=True)
                last.then_inc(B["out_mm"], 1)

            def outC(g):
                if is_first(g):
                    pe.wait_ge(s_val, 2)
                pe.wait_ge(C["aT"], g + 1)
                for k in range(GT):
                    b, t = k // 2, k % 2
                    last = pe.matmul(bank[1][:, k * P:(k + 1) * P], aTC[:, b, t * P:(t + 1) * P], keys_of(values, g),
                                     start=True, stop=True)
                last.then_inc(C["out_mm"], 1)

            def turn_keys():
                pe.wait_ge(s_ident, 1)
                pe.wait_ge(ld_ctx, 16)
                for g in range(NG):
                    last = pe.transpose(bank[4 + g // 4][:, g % 4 * P:(g % 4 + 1) * P], CTX[:, g * P:(g + 1) * P], ident[:, :])
                    if g % 4 == 3:
                        last.then_inc(s_cT_mm, 1)

            def turn_rows():
                pe.wait_ge(ld_rows, 96)
                pe.transpose(bank[6][:, 0:13], rows[:, :], ident[0:13, 0:13]).then_inc(s_rowsT, 1)

            def outputs_of_keys():
                pe.wait_ge(ld_qv, 16)
                pe.wait_ge(s_cT, 2)
                for g in range(NG):
                    last = pe.matmul(bank[(3, 5)[g // 4]][:, g % 4 * P:(g % 4 + 1) * P], cT[:, g * P:(g + 1) * P],
                                     wqv[:, 1, :], start=True, stop=True)
                    if g % 4 == 3:
                        last.then_inc(s_cw2_mm, 1)

            def keys_times_w2():
                pe.wait_ge(s_w2rep, 1)
                pe.wait_ge(s_cols, 1)
                pe.wait_ge(s_cT, 2)
                for half, dst in enumerate((bank[6], bank[1])):
                    pe.matmul(dst[:, :], w2_rep[:, :], cT[:, half * 512:(half + 1) * 512], start=True, stop=True)\
                        .then_inc(s_rkey_mm, 1)

            def weights_of_keys():
                pe.wait_ge(s_ident, 1)
                pe.wait_ge(ld_proj, 48)
                pe.matmul(bank[7][:, 0:P], wk[:, :], wq[:, :], start=True, stop=True)
                pe.transpose(bank[7][:, P:2 * P], wv[:, :], ident[:, :]).then_inc(s_wk_mm, 1)

            def project_keys():
                pe.wait_ge(s_wk, 2)
                pe.wait_ge(s_cT, 2)
                pe.wait_ge(s_rkey, 2)
                pe.wait_ge(s_cw2, 2)
                for half, dst in enumerate((bank[1], bank[3])):
                    pe.matmul(dst[:, :], wkq[:, :], cT[:, half * 512:(half + 1) * 512], start=True, stop=True)\
                        .then_inc(s_proj_mm, 1)

            def values_of_keys():
                pe.wait_ge(s_wk, 2)
                pe.wait_ge(s_cT, 2)
                pe.wait_ge(s_rkey, 2)
                pe.wait_ge(s_cw2, 2)
                for g in range(NG):
                    last = pe.matmul(bank[5 + g // 4][:, g % 4 * P:(g % 4 + 1) * P], cT[:, g * P:(g + 1) * P], wvT[:, :],
                                     start=True, stop=True)
                    if g % 4 == 3:
                        last.then_inc(s_val_mm, 1)

            def sum_partitions():
                pe.wait_ge(s_absum, 2)
                pe.wait_ge(s_val, 2)
                pe.matmul(bank[6][:, 16:18], ones[:, :], absum[:, :], start=True, stop=True).then_inc(s_absum_mm, 1)

            def turn_up_weights():
                pe.wait_ge(s_quant, 1)
                pe.wait_ge(s_gamma, 1)
                for c in range(HC):
                    last = pe.transpose(bank[6][:, c * P:(c + 1) * P], wfc[:, c, :], ident[:, :])
                last.then_inc(s_fcT, 1)

            def turn_down_weights():
                pe.wait_ge(s_val, 2)
                pe.wait_ge(s_quant, 2)
                for c in range(HC):
                    last = pe.transpose(bank[5][:, c * P:(c + 1) * P], wpj[:, c, :], ident[:, :])
                last.then_inc(s_pjT, 1)

            def norm_bias_through_projection():
                pe.wait_ge(s_pjT_cp, 1)
                pe.wait_ge(s_fcT_cp, 1)
                pe.wait_ge(s_lnb, HC)
                for c in range(HC):
                    last = pe.matmul(bank[6][:, 0:P], lnb_rep[:, c, :], wpjT[:, c, :], start=(c == 0), stop=(c == HC - 1))
                last.then_inc(s_ob, 1)

            def up(g, k):
                pe.wait_ge(Dd["lo"], g + 1)
                if k >= 2:
                    pe.wait_ge(Dd["gel"], GT * g + k - 1)
                elif k == 1:
                    before(pe, Dd["gel"], g, GT)
                    if is_first(g):
                        pe.wait_ge(A["prod"], NG)
                o = bank[2 + 2 * (k % 2)][:, :]
                pe.matmul(o, hiD[:, k * P:(k + 1) * P], wfcT[:, :], start=True, stop=False)
                pe.matmul(o, loD[:, k * P:(k + 1) * P], wfcT[:, :], start=False, stop=True).then_inc(Dd["fc_mm"], 1)

            def turn(g, k):
                if k in DVE_TILES:
                    pe.wait_ge(E["gnV"], NV * g + DVE_TILES.index(k) + 1)
                else:
                    pe.wait_ge(E["gnA"], NA * g + ACT_TILES.index(k) + 1)
                if k >= 1:
                    pe.wait_ge(E["gT"], GT * g + k)
                else:
                    before(pe, E["gT"], g, GT)
                    if is_first(g):
                        pe.wait_ge(A["xT"], NG)
                for c in range(HC):
                    last = pe.transpose(bank[0][:, c * P:(c + 1) * P], gn[:, k, c * P:(c + 1) * P], ident[:, :])
                last.then_inc(E["gT_mm"], 1)

            def down(g, k):
                pe.wait_ge(E["gT"], GT * g + k + 1)
                if k == 0:
                    before(pe, E["x"], g)
                    if is_first(g):
                        pe.wait_ge(A["x"], NG)
                        pe.wait_ge(s_pjln, HC)
                for c in range(HC):
                    last = pe.matmul(bank[7][:, k * P:(k + 1) * P], gnT[:, k, c * P:(c + 1) * P], wpjT_ln[:, c, :],
                                     start=(c == 0), stop=(c == HC - 1))
                last.then_inc(E["out_mm"], 1)

            turn_keys()
            weights_of_keys()
            turn_rows()
            outputs_of_keys()
            xT(A, nA, bank[0], 0)
            keys_times_w2()
            scores(A, xTA, simkey, bank[2], 0)
            values_of_keys()
            turn_max(0)
            spread_max(0)
            batch_sums(0)
            sum_partitions()
            aT(A, aA, bank[2], 0)
            attended(0)
            xT(A, nA, bank[0], 1)
            outA(0, 0)
            outA(0, 1)
            outA(0, 2)
            outA(0, 3)
            turn_up_weights()
            turn_down_weights()
            scores(A, xTA, simkey, bank[2], 1)
            project_keys()
            turn_max(1)
            spread_max(1)
            norm_bias_through_projection()
            aT(A, aA, bank[2], 1)
            batch_sums(1)
            xT(B, nB, bank[5], 0)
            attended(1)
            inner(0)
            outA(1, 0)
            outA(1, 1)
            outA(1, 2)
            outA(1, 3)
            xT(A, nA, bank[0], 2)
            sum_units(0, 0)
            scores(A, xTA, simkey, bank[2], 2)
            sum_units(0, 1)
            sum_units(0, 2)
            turn_max(2)
            sum_units(0, 3)
            spread_max(2)
            outB(0)
            aT(A, aA, bank[2], 2)
            batch_sums(2)
            xT(B, nB, bank[5], 1)
            attended(2)
            inner(1)
            outA(2, 0)
            outA(2, 1)
            outA(2, 2)
            outA(2, 3)
            xT(A, nA, bank[0], 3)
            sum_units(1, 0)
            xT(C, nC, bank[1], 0)
            scores(A, xTA, simkey, bank[2], 3)
            scores(C, xTC, projkey, bank[3], 0)
            sum_units(1, 1)
            sum_units(1, 2)
            turn_max(3)
            sum_units(1, 3)
            spread_max(3)
            outB(1)
            aT(C, aC, bank[3], 0)
            batch_sums(3)
            outC(0)
            aT(A, aA, bank[2], 3)
            xT(B, nB, bank[5], 2)
            attended(3)
            inner(2)
            with pe.Fori(K + 1, NG) as i:
                outA(i - 1, 0)
                outA(i - 1, 1)
                outA(i - 1, 2)
                xT(C, nC, bank[1], i - 3)
                outA(i - 1, 3)
                xT(A, nA, bank[0], i)
                scores(C, xTC, projkey, bank[3], i - 3)
                scores(A, xTA, simkey, bank[2], i)
                sum_units(i - 2, 0)
                sum_units(i - 2, 1)
                sum_units(i - 2, 2)
                turn_max(i)
                sum_units(i - 2, 3)
                spread_max(i)
                outB(i - 2)
                aT(C, aC, bank[3], i - 3)
                batch_sums(i)
                outC(i - 3)
                aT(A, aA, bank[2], i)
                xT(B, nB, bank[5], i - 1)
                attended(i)
                inner(i - 1)
            outA(7, 0)
            outA(7, 1)
            outA(7, 2)
            outA(7, 3)
            xT(C, nC, bank[1], 5)
            sum_units(6, 0)
            xT(Dd, nD, bank[2], 0)
            scores(C, xTC, projkey, bank[3], 5)
            sum_units(6, 1)
            up(0, 0)
            up(0, 1)
            sum_units(6, 2)
            sum_units(6, 3)
            up(0, 2)
            up(0, 3)
            outB(6)
            xT(B, nB, bank[5], 7)
            aT(C, aC, bank[3], 5)
            xT(Dd, nD, bank[2], 1)
            inner(7)
            outC(5)
            up(1, 0)
            sum_units(7, 0)
            sum_units(7, 1)
            up(1, 1)
            up(1, 2)
            turn(0, 0)
            xT(C, nC, bank[1], 6)
            sum_units(7, 2)
            down(0, 0)
            up(1, 3)
            scores(C, xTC, projkey, bank[3], 6)
            turn(0, 1)
            sum_units(7, 3)
            outB(7)
            xT(Dd, nD, bank[2], 2)
            turn(0, 2)
            down(0, 1)
            down(0, 2)
            aT(C, aC, bank[3], 6)
            turn(0, 3)
            up(2, 0)
            outC(6)
            up(2, 1)
            turn(1, 0)
            xT(C, nC, bank[1], 7)
            up(2, 2)
            scores(C, xTC, projkey, bank[3], 7)
            down(0, 3)
            up(2, 3)
            down(1, 0)
            aT(C, aC, bank[3], 7)
            turn(1, 1)
            xT(Dd, nD, bank[2], 3)
            outC(7)
            with pe.Fori(K2 + 1, NG) as i:
                turn(i - 3, 2)
                down(i - 3, 1)
                turn(i - 3, 3)
                down(i - 3, 2)
                down(i - 3, 3)
                up(i - 1, 0)
                up(i - 1, 1)
                turn(i - 2, 0)
                up(i - 1, 2)
                up(i - 1, 3)
                turn(i - 2, 1)
                down(i - 2, 0)
                xT(Dd, nD, bank[2], i)
            turn(5, 2)
            down(5, 1)
            turn(5, 3)
            up(7, 0)
            down(5, 2)
            turn(6, 0)
            up(7, 1)
            up(7, 2)
            turn(6, 1)
            down(5, 3)
            up(7, 3)
            turn(6, 2)
            down(6, 0)
            down(6, 1)
            turn(6, 3)
            down(6, 2)
            down(6, 3)
            turn(7, 0)
            turn(7, 1)
            down(7, 0)
            turn(7, 2)
            down(7, 1)
            turn(7, 3)
            down(7, 2)
            down(7, 3)


_INS = ["x", "ctx_1024", "L0_xattn_w_sim", "L0_xattn_b_sim", "L0_xattn_W_qv", "L0_xattn_b_qv", "L0_ffn_Win",
        "L0_ffn_bin_", "L0_ffn_W1", "L0_ffn_b1", "L0_ffn_W2", "L0_ffn_b2", "L0_ffn_Wout", "L0_ffn_bout",
        "L1_xattn_WQ", "L1_xattn_WK", "L1_xattn_WV", "L1_ffn_W_fc", "L1_ffn_ln_w", "L1_ffn_ln_b",
        "L1_ffn_W_proj"]


def kernel(**inputs):
    import numpy as np
    import concourse.bacc as bacc
    from concourse.bass_utils import run_bass_kernel_spmd

    nc = bacc.Bacc("TRN2", target_bir_lowering=False, num_devices=1)
    arrays, args = {}, []
    for name in _INS:
        a = np.ascontiguousarray(inputs[name])
        arrays[f"in_{name}"] = a
        args.append(nc.dram_tensor(f"in_{name}", a.shape, mybir.dt.from_np(a.dtype), kind="ExternalInput").ap())
    shape = inputs["x"].shape
    out = nc.dram_tensor("out_0", shape, F32, kind="ExternalOutput").ap()
    xattn_ffn_stack(nc, *args, out)
    r = run_bass_kernel_spmd(nc, [arrays], core_ids=[0])
    return r.results[0]["out_0"]
```
